# Optimizing a Trainium2 kernel written in Bass

```python
import numpy as np
import jax
import jax.numpy as jnp

def _softmax(x, axis=-1):
    return jax.nn.softmax(x, axis=axis)

def _gelu(x):
    return jax.nn.gelu(x, approximate=True)

def _silu(x):
    return jax.nn.silu(x)

def _sigmoid(x):
    return jax.nn.sigmoid(x)

def _layernorm(x, axis=-1, eps=1e-05):
    m = jnp.mean(x, axis=axis, keepdims=True)
    v = jnp.var(x, axis=axis, keepdims=True)
    return (x - m) / jnp.sqrt(v + eps)

def _scatter_add(tgt, idx, src, axis=0):
    return tgt.at[idx].add(src)

def _segment_sum(src, seg, n):
    return jax.ops.segment_sum(src, seg, n)
kernel_name = 'mk_adj_resnorm_d1_adj_r2_44ead8'

def setup_inputs(seed: int=0):
    np.random.seed(seed)
    _w = jnp.asarray

    def _rec_inputs():
        import jax
        import jax.numpy as jnp
        _gk = jax.random.key(seed)
        x = -1.394e-06 + 0.9999 * jax.random.normal(jax.random.fold_in(_gk, 1), (4096, 256), jnp.float32)
        _a = jax.random.bernoulli(jax.random.fold_in(_gk, 2), 0.000976562, (4096, 4096))
        _a = jnp.logical_or(_a, jnp.swapaxes(_a, -1, -2))
        _a = jnp.logical_or(_a, jnp.eye(4096, dtype=bool))
        adj = _a
        return (x, adj)
    x, adj = _rec_inputs()

    def _L0_gnn_setup():
        import jax, jax.numpy as jnp
        import numpy as np
        import math
        N = 4096
        D_IN = 256
        LOCAL_D = 256
        GLOBAL_D = 256
        key = jax.random.key(seed)
        ks = jax.random.split(key, 16)
        s = 1.0 / math.sqrt(D_IN)
        adj = jax.random.bernoulli(ks[0], 0.01, (N, N))
        adj = adj | jnp.eye(N, dtype=bool)
        return {'adj_matrix': adj, 'x': jax.random.normal(ks[1], (N, D_IN), jnp.float32), 'masked_x': jax.random.normal(ks[2], (N, D_IN), jnp.float32), 'Wlq': jax.random.normal(ks[3], (D_IN, LOCAL_D), jnp.float32) * s, 'Wlk': jax.random.normal(ks[4], (D_IN, LOCAL_D), jnp.float32) * s, 'Wlv': jax.random.normal(ks[5], (D_IN, D_IN), jnp.float32) * s, 'blv': jax.random.normal(ks[6], (D_IN,), jnp.float32) * 0.01, 'Wgq': jax.random.normal(ks[7], (D_IN, GLOBAL_D), jnp.float32) * s, 'Wgk': jax.random.normal(ks[8], (D_IN, GLOBAL_D), jnp.float32) * s, 'Wgv': jax.random.normal(ks[9], (D_IN, D_IN), jnp.float32) * s, 'bgv': jax.random.normal(ks[10], (D_IN,), jnp.float32) * 0.01, 'Wes': jax.random.normal(ks[11], (D_IN, 1), jnp.float32) * s, 'Wev': jax.random.normal(ks[12], (D_IN, D_IN), jnp.float32) * s, 'bev': jax.random.normal(ks[13], (D_IN,), jnp.float32) * 0.01}
    _L0_gnn_all = _L0_gnn_setup()
    _L0_gnn_in = {k: v for k, v in _L0_gnn_all.items() if k in ('masked_x', 'Wlq', 'Wlk', 'Wlv', 'blv', 'Wgq', 'Wgk', 'Wgv', 'bgv', 'Wes', 'Wev', 'bev')}
    del _L0_gnn_all
    return {'x': x, 'adj': adj, 'L0_gnn_masked_x': _L0_gnn_in['masked_x'], 'L0_gnn_Wlq': _L0_gnn_in['Wlq'], 'L0_gnn_Wlk': _L0_gnn_in['Wlk'], 'L0_gnn_Wlv': _L0_gnn_in['Wlv'], 'L0_gnn_blv': _L0_gnn_in['blv'], 'L0_gnn_Wgq': _L0_gnn_in['Wgq'], 'L0_gnn_Wgk': _L0_gnn_in['Wgk'], 'L0_gnn_Wgv': _L0_gnn_in['Wgv'], 'L0_gnn_bgv': _L0_gnn_in['bgv'], 'L0_gnn_Wes': _L0_gnn_in['Wes'], 'L0_gnn_Wev': _L0_gnn_in['Wev'], 'L0_gnn_bev': _L0_gnn_in['bev']}

def reference(x, adj, L0_gnn_masked_x, L0_gnn_Wlq, L0_gnn_Wlk, L0_gnn_Wlv, L0_gnn_blv, L0_gnn_Wgq, L0_gnn_Wgk, L0_gnn_Wgv, L0_gnn_bgv, L0_gnn_Wes, L0_gnn_Wev, L0_gnn_bev):
    import jax
    import jax.numpy as jnp

    def _L0_gnn_ref(adj_matrix, x, masked_x, Wlq, Wlk, Wlv, blv, Wgq, Wgk, Wgv, bgv, Wes, Wev, bev):
        import jax, jax.numpy as jnp
        import numpy as np
        import math
        N = 4096
        D_IN = 256
        LOCAL_D = 256
        GLOBAL_D = 256
        scale = 1.0 / math.sqrt(D_IN)
        x_bar = jnp.mean(x, axis=0, keepdims=True)
        lQ = masked_x @ Wlq
        lK = x @ Wlk
        lV = x @ Wlv + blv
        gQ = masked_x @ Wgq
        gK = x_bar @ Wgk
        gV = x_bar @ Wgv + bgv
        es = masked_x @ Wes
        eV = masked_x @ Wev + bev
        local_scores = lQ @ lK.T * scale
        local_scores = jnp.where(adj_matrix, local_scores, jnp.float32(-1000000000.0))
        global_scores = gQ @ gK.T * scale
        max_score = jnp.maximum(jnp.max(local_scores, axis=1, keepdims=True), jnp.maximum(global_scores, es))
        le = jnp.exp(local_scores - max_score)
        ge = jnp.exp(global_scores - max_score)
        ee = jnp.exp(es - max_score)
        denom = jnp.sum(le, axis=-1, keepdims=True) + ge + ee
        res = le / denom @ lV + ge / denom * gV + ee / denom * eV
        x_recon = jnp.maximum(res, masked_x)
        return x_recon
    x = _layernorm(x + _L0_gnn_ref(adj, x, L0_gnn_masked_x, L0_gnn_Wlq, L0_gnn_Wlk, L0_gnn_Wlv, L0_gnn_blv, L0_gnn_Wgq, L0_gnn_Wgk, L0_gnn_Wgv, L0_gnn_bgv, L0_gnn_Wes, L0_gnn_Wev, L0_gnn_bev), axis=-1)
    return x

_drawn_inputs = setup_inputs


def setup_inputs(seed=0):
    import zlib

    import numpy as np

    out = dict(_drawn_inputs(seed))
    spreads = {}
    factors = {'L0_gnn_blv': 8.0,
     'L0_gnn_Wgq': 8.0,
     'L0_gnn_Wgk': 8.0,
     'L0_gnn_Wgv': 50.544,
     'L0_gnn_bgv': 64.0,
     'L0_gnn_bev': 64.0}
    for name, (base, spread) in spreads.items():
        noise = np.random.default_rng([zlib.crc32(name.encode()), seed]).standard_normal(out[name].shape)
        drawn = base * np.exp(spread * noise) if base else spread * noise
        out[name] = jnp.asarray(drawn.astype(out[name].dtype))
    for name, factor in factors.items():
        out[name] = (out[name] * factor).astype(out[name].dtype)
    return out
```

```python
import concourse.bass as bass
from concourse import mybir
from concourse.alu_op_type import AluOpType as ALU
from contextlib import ExitStack

FP32 = mybir.dt.float32
F32R = mybir.dt.float32r
U8 = mybir.dt.uint8
ACT = mybir.ActivationFunctionType
AX = mybir.AxisListType.X
RMAX = bass.bass_isa.ReduceOp.max

P = 128
N = 4096
D = 256
DC = D // P
KT = N // P
QB = 256
NB = N // QB
QT = QB // P
GK = 4
GW = GK * QB
GB = KT // GK
CG = GB // 2
NG = NB * GB
VW = D + 2
EW = D + 2
OW = D + 3
LAG_SHIFT = 5
LAG_LOW = 6
LAG_PV = 7
LW = 512
NL = N // LW
SCALE = 1.0 / 16.0
MASKED = -1e9
EPS = 1e-5


def started(v):
    return not isinstance(v, int) or v > 0


def build(nc, x, xT, mxT, mx, mask, w, out):
    ctx = ExitStack()
    with ctx:
        def sb(name, shape, dt, to=ctx):
            return to.enter_context(nc.sbuf_tensor(name, shape, dt))

        def pb(name, shape, to=ctx):
            return to.enter_context(nc.psum_tensor(name, shape, FP32))

        def sem(name):
            return ctx.enter_context(nc.semaphore(name))

        q_dram = nc.dram_tensor("q_split", (NB, P, 2, DC, QB), FP32, kind="Internal").ap()
        e_dram = nc.dram_tensor("self_values", (NB, P, QT, EW), FP32, kind="Internal").ap()

        k_hi = sb("k_hi", [P, DC, N], F32R)
        k_lo = sb("k_lo", [P, DC, N], F32R)
        v_hi = sb("v_hi", [P, KT, VW], F32R)
        v_lo = sb("v_lo", [P, KT, D], F32R)
        g_val = sb("g_val", [P, D], FP32)
        one = sb("one", [P, 4], FP32)
        consts = sb("consts", [P, 4], FP32)

        prologue(nc, sb, pb, sem, xT, mxT, w, q_dram, e_dram, k_hi, k_lo, v_hi, v_lo, g_val, one, consts)
        attention(nc, sb, pb, sem, x, mx, mask, out, q_dram, e_dram, k_hi, k_lo, v_hi, v_lo, g_val, one, consts)


def prologue(nc, sb, pb, sem, xT, mxT, w, q_dram, e_dram, k_hi, k_lo, v_hi, v_lo, g_val, one, consts):
    own = ExitStack()
    with own:
        stage = sb("stage", [P, 2, DC, LW], FP32, own)
        m_hi = sb("m_hi", [P, 2, DC, LW], F32R, own)
        m_lo = sb("m_lo", [P, 2, DC, LW], F32R, own)
        wlq = sb("wlqT", [P, DC, D], FP32, own)
        wlk = sb("wlkT", [P, DC, D], FP32, own)
        wgq = sb("wgqT", [P, DC, D], FP32, own)
        wgk = sb("wgk", [P, DC, D], FP32, own)
        wgv = sb("wgv", [P, DC, D], FP32, own)
        wlv = sb("wlv", [P, DC, D], FP32, own)
        wlv_hi = sb("wlv_hi", [P, DC, D], F32R, own)
        wlv_lo = sb("wlv_lo", [P, DC, D], F32R, own)
        wev = sb("wev", [P, DC, EW], FP32, own)
        wev_hi = sb("wev_hi", [P, DC, EW], F32R, own)
        wev_lo = sb("wev_lo", [P, DC, EW], F32R, own)
        mm_hi = sb("mm_hi", [P, DC, D], F32R, own)
        mm_lo = sb("mm_lo", [P, DC, D], F32R, own)
        blv = sb("blv", [P, D], FP32, own)
        bev = sb("bev", [P, EW], FP32, own)
        bgv = sb("bgv", [P, D], FP32, own)
        v_raw = sb("v_raw", [P, 2, D], FP32, own)
        q_out = sb("q_out", [P, 2, DC, LW], F32R, own)
        e_out = sb("e_out", [P, LW // P, EW], FP32, own)
        x_sum = sb("x_sum", [P, DC, NL], FP32, own)
        x_bar = sb("x_bar", [P, DC], FP32, own)
        x_wide = sb("x_wide", [P, DC, P], FP32, own)
        g_key = sb("g_key", [P, DC], FP32, own)

        m_ps = pb("m_ps", [P, DC, D], own)
        v_ps = pb("v_ps", [P, 2, 2, D], own)
        q_ps = pb("q_ps", [P, DC, LW], own)
        e_ps = pb("e_ps", [P, 2, 512], own)
        g_ps = pb("g_ps", [P, 512], own)

        weights_in = sem("weights_in")
        staged = [sem("staged_even"), sem("staged_odd")]
        tidy = sem("tidy")
        wlv_split, wev_split = sem("wlv_split"), sem("wev_split")
        mm_made, mm_hi_done, mm_split = sem("mm_made"), sem("mm_hi_done"), sem("mm_split")
        key_hi, key_lo = sem("key_hi"), sem("key_lo")
        v_made, v_added, v_hi_done, v_lo_done = sem("v_made"), sem("v_added"), sem("v_hi_done"), sem("v_lo_done")
        mean_made, g_key_made, g_key_in, g_score_made = sem("mean_made"), sem("g_key_made"), sem("g_key_in"), sem("g_score_made")
        g_val_made, g_val_done = sem("g_val_made"), sem("g_val_done")
        m_hi_done, m_lo_done = sem("m_hi_done"), sem("m_lo_done")
        q_made, q_hi_done, q_lo_done = sem("q_made"), sem("q_hi_done"), sem("q_lo_done")
        e_made, e_done = sem("e_made"), sem("e_done")
        q_stored, e_stored = sem("q_stored"), sem("e_stored")
        NW = 12
        VT = KT // 2
        LT = LW // P

        block = own.enter_context(nc.Block())

        @block.sync
        def _(sp):
            rows = "(c p) n -> p c n"
            sp.dma_start(wlq[:], w["WlqT"].rearrange(rows, p=P)).then_inc(weights_in, 16)
            sp.dma_start(wlk[:], w["WlkT"].rearrange(rows, p=P)).then_inc(weights_in, 16)
            xs = xT.rearrange("(c p) (l n) -> l p c n", p=P, n=LW)
            ms = mxT.rearrange("(c p) (l n) -> l p c n", p=P, n=LW)
            for i in range(NL):
                if i >= 2:
                    sp.wait_ge(key_hi, DC * (i - 1))
                    sp.wait_ge(key_lo, i - 1)
                sp.dma_start(stage[:, i % 2], xs[i]).then_inc(staged[i % 2], 16)
            for i in range(NL):
                sp.wait_ge(key_hi, DC * min(NL, NL + i - 1))
                sp.wait_ge(key_lo, min(NL, NL + i - 1))
                if i >= 2:
                    sp.wait_ge(m_lo_done, i - 1)
                sp.dma_start(stage[:, i % 2], ms[i]).then_inc(staged[i % 2], 16)

        @block.scalar
        def _(act):
            rows = "(c p) n -> p c n"
            act.dma_start(wlv[:], w["Wlv"].rearrange(rows, p=P)).then_inc(weights_in, 16)
            act.dma_start(blv[:], w["blv"].rearrange("(a n) -> a n", a=1).broadcast_to([P, D])).then_inc(weights_in, 16)
            act.dma_start(wgk[:], w["Wgk"].rearrange(rows, p=P)).then_inc(weights_in, 16)
            act.dma_start(wgq[:], w["WgqT"].rearrange(rows, p=P)).then_inc(weights_in, 16)
            act.dma_start(wgv[:], w["Wgv"].rearrange(rows, p=P)).then_inc(weights_in, 16)
            act.dma_start(bgv[:], w["bgv"].rearrange("(a n) -> a n", a=1).broadcast_to([P, D])).then_inc(weights_in, 16)
            act.dma_start(wev[:, :, 0:D], w["Wev"].rearrange(rows, p=P)).then_inc(weights_in, 16)
            act.dma_start(wev[:, 0, D:D + 1], w["Wes"][0:P, :]).then_inc(weights_in, 16)
            act.dma_start(wev[:, 1, D:D + 1], w["Wes"][P:D, :]).then_inc(weights_in, 16)
            act.dma_start(bev[:, 0:D], w["bev"].rearrange("(a n) -> a n", a=1).broadcast_to([P, D])).then_inc(weights_in, 16)
            act.wait_ge(weights_in, 16 * NW)
            nc.scalar.activation(wlv_hi[:], wlv[:], ACT.Copy).then_inc(wlv_split, 1)
            act.wait_ge(mm_made, 1)
            nc.scalar.activation(mm_hi[:], m_ps[:], ACT.Copy, scale=SCALE).then_inc(mm_hi_done, 1)
            for i in range(NL):
                act.wait_ge(staged[i % 2], 16 * (i // 2 + 1))
                for c in range(DC):
                    nc.scalar.activation(k_hi[:, c, LW * i:LW * (i + 1)], stage[:, i % 2, c], ACT.Copy,
                                         accum_out=x_sum[:, c, i:i + 1]).then_inc(key_hi, 1)
                if i:
                    for t in range(2 * (i - 1), 2 * i):
                        act.wait_ge(v_added, t + 1)
                        nc.scalar.activation(v_hi[:, 2 * t:2 * t + 2, 0:D], v_raw[:], ACT.Copy).then_inc(v_hi_done, 1)
            for t in range(VT - 2, VT):
                act.wait_ge(v_added, t + 1)
                nc.scalar.activation(v_hi[:, 2 * t:2 * t + 2, 0:D], v_raw[:], ACT.Copy).then_inc(v_hi_done, 1)
            act.wait_ge(g_score_made, 2)
            act.wait_ge(wev_split, 2)
            nc.scalar.activation(wev_hi[:], wev[:], ACT.Copy).then_inc(wev_split, 1)
            for i in range(NL):
                act.wait_ge(staged[i % 2], 16 * ((NL + i) // 2 + 1))
                if i >= 2:
                    act.wait_ge(e_made, LT * (i - 1))
                nc.scalar.activation(m_hi[:, i % 2], stage[:, i % 2], ACT.Copy).then_inc(m_hi_done, 1)
                act.wait_ge(q_made, i + 1)
                if i:
                    act.wait_ge(q_stored, 64 * i)
                nc.scalar.activation(q_out[:, 0], q_ps[:], ACT.Copy).then_inc(q_hi_done, 1)
                act.wait_ge(q_lo_done, i + 1)
                act.wait_ge(q_hi_done, i + 1)
                for h in range(LW // QB):
                    for part in range(2):
                        act.dma_start(q_dram[i * (LW // QB) + h][:, part],
                                      q_out[:, part, :, QB * h:QB * (h + 1)].bitcast(FP32)).then_inc(q_stored, 16)
            act.wait_ge(q_stored, 64 * NL)

        @block.gpsimd
        def _(pool):
            nc.gpsimd.memset(one[:], 1.0).then_inc(tidy, 1)
            nc.gpsimd.memset(consts[:, 0:2], -0.5).then_inc(tidy, 1)
            nc.gpsimd.memset(consts[:, 2:4], 1.0).then_inc(tidy, 1)
            nc.gpsimd.memset(bev[:, D:EW], 0.0).then_inc(tidy, 1)
            for i in range(NL):
                pool.wait_ge(e_done, LT * (i + 1))
                for h in range(LW // QB):
                    pool.dma_start(e_dram[i * (LW // QB) + h], e_out[:, QT * h:QT * (h + 1)]).then_inc(e_stored, 16)
            pool.wait_ge(e_stored, 32 * NL)

        @block.vector
        def _(dve):
            dve.wait_ge(tidy, 4)
            nc.vector.tensor_copy(v_hi[:, :, D:VW], one[:, 0:2].unsqueeze(1).broadcast_to([P, KT, 2])).then_inc(tidy, 1)
            dve.wait_ge(weights_in, 16 * NW)
            dve.wait_ge(wlv_split, 1)
            nc.vector.tensor_tensor(wlv_lo[:], wlv[:], wlv_hi[:], ALU.subtract).then_inc(wlv_split, 1)
            dve.wait_ge(mm_hi_done, 1)
            nc.vector.scalar_tensor_tensor(mm_lo[:], m_ps[:], SCALE, mm_hi[:], ALU.mult, ALU.subtract).then_inc(mm_split, 1)

            def values(t):
                dve.wait_ge(v_made, t + 1)
                if t:
                    dve.wait_ge(v_hi_done, t)
                    dve.wait_ge(v_lo_done, t)
                nc.vector.tensor_tensor(v_raw[:], v_ps[:, t % 2], blv[:].unsqueeze(1).broadcast_to([P, 2, D]),
                                        ALU.add).then_inc(v_added, 1)
                dve.wait_ge(v_added, t + 1)
                dve.wait_ge(v_hi_done, t + 1)
                nc.vector.tensor_tensor(v_lo[:, 2 * t:2 * t + 2], v_raw[:], v_hi[:, 2 * t:2 * t + 2, 0:D],
                                        ALU.subtract).then_inc(v_lo_done, 1)

            for i in range(NL):
                dve.wait_ge(key_hi, DC * (i + 1))
                nc.vector.tensor_tensor(k_lo[:, :, LW * i:LW * (i + 1)], stage[:, i % 2],
                                        k_hi[:, :, LW * i:LW * (i + 1)], ALU.subtract).then_inc(key_lo, 1)
                if i:
                    for t in range(2 * (i - 1), 2 * i):
                        values(t)
            nc.vector.tensor_reduce(x_bar[:], x_sum[:], AX, ALU.add).then_inc(mean_made, 1)
            dve.wait_ge(mean_made, 1)
            nc.vector.tensor_scalar(x_bar[:], x_bar[:], 1.0 / N, None, ALU.mult).then_inc(mean_made, 1)
            dve.wait_ge(mean_made, 2)
            nc.vector.tensor_copy(x_wide[:], x_bar[:].unsqueeze(2).broadcast_to([P, DC, P])).then_inc(mean_made, 1)
            for t in range(VT - 2, VT):
                values(t)
            dve.wait_ge(g_key_made, 1)
            nc.vector.tensor_copy(g_key[:], g_ps[:, 0:DC]).then_inc(g_key_in, 1)
            dve.wait_ge(g_score_made, 1)
            nc.vector.tensor_scalar(wev[:, :, D + 1:D + 2], g_ps[:, 2:2 + DC].unsqueeze(2), SCALE, None,
                                    ALU.mult).then_inc(g_score_made, 1)
            dve.wait_ge(g_val_made, 1)
            nc.vector.tensor_tensor(g_val[:], g_ps[:, 16:16 + D], bgv[:], ALU.add).then_inc(wev_split, 2)
            dve.wait_ge(wev_split, 3)
            nc.vector.tensor_tensor(wev_lo[:], wev[:], wev_hi[:], ALU.subtract).then_inc(wev_split, 1)
            for i in range(NL):
                dve.wait_ge(m_hi_done, i + 1)
                if i >= 2:
                    dve.wait_ge(e_made, LT * (i - 1))
                nc.vector.tensor_tensor(m_lo[:, i % 2], stage[:, i % 2], m_hi[:, i % 2], ALU.subtract).then_inc(m_lo_done, 1)
                dve.wait_ge(q_hi_done, i + 1)
                nc.vector.tensor_tensor(q_out[:, 1], q_ps[:], q_out[:, 0], ALU.subtract).then_inc(q_lo_done, 1)
                for t in range(LT):
                    dve.wait_ge(e_made, LT * i + t + 1)
                    if i:
                        dve.wait_ge(e_stored, 32 * i)
                    nc.vector.tensor_tensor(e_out[:, t], e_ps[:, t % 2, 0:EW], bev[:], ALU.add).then_inc(e_done, 1)

        @block.tensor
        def _(pe):
            def product(out, hi, lo, rhs_hi, rhs_lo):
                steps = [(c, a, b) for c in range(DC) for a, b in ((hi, rhs_hi), (hi, rhs_lo), (lo, rhs_hi))]
                for n, (c, a, b) in enumerate(steps):
                    last = nc.tensor.matmul(out, a(c), b(c), start=(n == 0), stop=(n == len(steps) - 1))
                return last

            pe.wait_ge(weights_in, 16 * NW)
            for i in range(DC):
                for c in range(DC):
                    last = nc.tensor.matmul(m_ps[:, i], wlq[:, c, P * i:P * (i + 1)], wlk[:, c],
                                            start=(c == 0), stop=(c == DC - 1))
            last.then_inc(mm_made, 1)
            pe.wait_ge(wlv_split, 2)
            for t in range(VT):
                if t % 2 == 0:
                    pe.wait_ge(key_lo, t // 2 + 1)
                if t >= 2:
                    pe.wait_ge(v_added, t - 1)
                for k in range(2 * t, 2 * t + 2):
                    at = slice(P * k, P * (k + 1))
                    last = product(v_ps[:, t % 2, k % 2], lambda c: k_hi[:, c, at], lambda c: k_lo[:, c, at],
                                   lambda c: wlv_hi[:, c], lambda c: wlv_lo[:, c])
                last.then_inc(v_made, 1)
            pe.wait_ge(mean_made, 2)
            for j in range(DC):
                for c in range(DC):
                    last = nc.tensor.matmul(g_ps[:, j:j + 1], wgk[:, c, P * j:P * (j + 1)], x_bar[:, c:c + 1],
                                            start=(c == 0), stop=(c == DC - 1))
            last.then_inc(g_key_made, 1)
            pe.wait_ge(g_key_in, 1)
            for j in range(DC):
                for c in range(DC):
                    last = nc.tensor.matmul(g_ps[:, 2 + j:3 + j], wgq[:, c, P * j:P * (j + 1)], g_key[:, c:c + 1],
                                            start=(c == 0), stop=(c == DC - 1))
            last.then_inc(g_score_made, 1)
            pe.wait_ge(mean_made, 3)
            pe.wait_ge(g_score_made, 2)
            for c in range(DC):
                last = nc.tensor.matmul(g_ps[:, 16:16 + D], x_wide[:, c], wgv[:, c], start=(c == 0), stop=(c == DC - 1))
            last.then_inc(g_val_made, 1)
            pe.wait_ge(mm_split, 1)
            pe.wait_ge(wev_split, 4)
            for i in range(NL):
                pe.wait_ge(m_hi_done, i + 1)
                pe.wait_ge(m_lo_done, i + 1)
                if i:
                    pe.wait_ge(q_lo_done, i)
                for j in range(DC):
                    at = slice(P * j, P * (j + 1))
                    last = product(q_ps[:, j], lambda c: mm_hi[:, c, at], lambda c: mm_lo[:, c, at],
                                   lambda c: m_hi[:, i % 2, c], lambda c: m_lo[:, i % 2, c])
                last.then_inc(q_made, 1)
                for t in range(LT):
                    at = slice(P * t, P * (t + 1))
                    if LT * i + t >= 2:
                        pe.wait_ge(e_done, LT * i + t - 1)
                    product(e_ps[:, t % 2, 0:EW], lambda c: m_hi[:, i % 2, c, at], lambda c: m_lo[:, i % 2, c, at],
                            lambda c: wev_hi[:, c], lambda c: wev_lo[:, c]).then_inc(e_made, 1)


def attention(nc, sb, pb, sem, x, mx, mask, out, q_dram, e_dram, k_hi, k_lo, v_hi, v_lo, g_val, one, consts):
    q_in = sb("q_in", [P, 2, 2, DC, QB], F32R)
    ring = sb("ring", [P, GB, GW], FP32)
    mask_in = sb("mask_in", [P, 2, 2 * GW], U8)
    p_hi = sb("p_hi", [P, 2, GW], F32R)
    p_lo = sb("p_lo", [P, 2, GW], F32R)
    top = sb("top", [P, GW], FP32)
    c_max = sb("c_max", [P, 2, QB], FP32)
    o_in = sb("o_in", [P, 2, QT, OW + 1], FP32)
    e_in = sb("e_in", [P, QT, EW], FP32)
    x_in = sb("x_in", [P, QT, D], FP32)
    mx_in = sb("mx_in", [P, QT, D], FP32)
    y_out = sb("y_out", [P, QT, D], FP32)
    tops = sb("tops", [P, QT, 4], FP32)
    neg_max = sb("neg_max", [P, QT], FP32)
    part_w = sb("part_w", [P, QT, 4], FP32)
    part_sum = sb("part_sum", [P, QT, 4], FP32)
    prod = sb("prod", [P, QT, 4], FP32)
    denom = sb("denom", [P, QT], FP32)
    rden = sb("rden", [P, QT], FP32)
    share = sb("share", [P, QT, 4], FP32)
    stats = sb("stats", [P, QT, 6], FP32)
    mean_var = sb("mean_var", [P, QT, 2], FP32)
    var_eps = sb("var_eps", [P, QT], FP32)
    rstd = sb("rstd", [P, QT], FP32)
    shift = sb("shift", [P, QT], FP32)

    s_ps = pb("s_ps", [P, 2, GW])
    o_ps = pb("o_ps", [P, 2, QT, 512])

    q_loaded, mask_loaded = sem("q_loaded"), [sem("mask_even"), sem("mask_odd")]
    e_loaded, rows_loaded, y_stored = sem("e_loaded"), sem("rows_loaded"), sem("y_stored")
    scores_ready, pv_done = sem("scores_ready"), sem("pv_done")
    slot_filled, chunk_max = sem("slot_filled"), sem("chunk_max")
    masked, top_steps, shifted, lo_ready = sem("masked"), sem("top_steps"), sem("shifted"), sem("lo_ready")
    exp_done, hi_ready = sem("exp_done"), sem("hi_ready")
    o_taken, part_w_ready, scaled, normed = sem("o_taken"), sem("part_w_ready"), sem("scaled"), sem("normed")
    negmax_steps, share_steps, merged, stat_steps, shift_ready = (
        sem("negmax_steps"), sem("share_steps"), sem("merged"), sem("stat_steps"), sem("shift_ready"))
    sums_ready = sem("sums_ready")
    summed, y_ready, rstd_steps = sem("summed"), sem("y_ready"), sem("rstd_steps")
    sp_passed, dve_passed, pool_passed = sem("sp_passed"), sem("dve_passed"), sem("pool_passed")
    TOPS = 5
    NEG, SHARE, STAT, SUMS = 4, 4, 4, 3

    def bodies(eng, body, first, last, end=NB):
        for b in range(first):
            body(b)
        with eng.Fori(first, end) as b:
            body(b)
        for b in range(end, last + 1):
            body(b)

    def held_apart(eng, count, passed):
        if not isinstance(count, int):
            eng.sem_inc(passed, 1)

    def group(b, j):
        g = b * GB + j
        return g if not isinstance(b, int) or 0 <= g < NG else None

    def ending(b, behind):
        return b - behind if not isinstance(b, int) or 0 <= b - behind < NB else None

    rows = "(b t p) d -> b p t d"
    x_rows, mx_rows, out_rows = (a.rearrange(rows, t=QT, p=P) for a in (x, mx, out))

    block = nc.Block()
    with block:
        @block.sync
        def _(sp):
            sp.dma_start(q_in[:, 0].bitcast(FP32), q_dram[0]).then_inc(q_loaded, 16)

            def body(b):
                here, one_back, two_back, three_back = (ending(b, n) for n in range(4))

                def mask_piece(m):
                    if started(GB * b + 2 * m - 2):
                        sp.wait_ge(masked, GB * b + 2 * m - 2)
                        held_apart(sp, b, sp_passed)
                    sp.dma_start(mask_in[:, m % 2], mask[b, m]).then_inc(mask_loaded[m % 2], 16)

                if here is not None:
                    mask_piece(0)
                if three_back is not None:
                    sp.wait_ge(normed, QT * (three_back + 1))
                    sp.dma_start(out_rows[three_back], y_out[:]).then_inc(y_stored, 16)
                if here is not None:
                    if not (isinstance(b, int) and b + 1 >= NB):
                        sp.wait_ge(q_loaded, 16 * (b + 1))
                        if started(GB * b):
                            sp.wait_ge(scores_ready, GB * b)
                        after = b + 1
                        sp.dma_start(q_in[:, bass.ds(after % 2, 1)].bitcast(FP32),
                                     q_dram[bass.ds(after, 1)].rearrange("a p h c n -> p a h c n")).then_inc(q_loaded, 16)
                    mask_piece(1)
                if two_back is not None:
                    if started(two_back):
                        sp.wait_ge(y_ready, two_back)
                    sp.dma_start(x_in[:], x_rows[two_back]).then_inc(rows_loaded, 16)
                    sp.dma_start(mx_in[:], mx_rows[two_back]).then_inc(rows_loaded, 16)
                if here is not None:
                    mask_piece(2)
                if one_back is not None:
                    if started(one_back):
                        sp.wait_ge(summed, SUMS * one_back)
                        held_apart(sp, b, sp_passed)
                        sp.wait_ge(e_loaded, 16 * one_back)
                    sp.dma_start(e_in[:], e_dram[one_back]).then_inc(e_loaded, 16)
                if here is not None:
                    mask_piece(3)
            bodies(sp, body, 3, NB + 2, NB - 1)
            sp.wait_ge(y_stored, 16 * NB)

        @block.tensor
        def _(pe):
            def scores(b, j):
                g = group(b, j)
                if g is None:
                    return
                if j == 0:
                    pe.wait_ge(q_loaded, 16 * (b + 1))
                if started(g - 1):
                    pe.wait_ge(masked, g - 1)
                par = b % 2
                for k in range(GK):
                    tile = GK * j + k
                    at = slice(P * tile, P * (tile + 1))
                    steps = [(c, a, h) for c in range(DC) for a, h in ((k_hi, 0), (k_hi, 1), (k_lo, 0))]
                    for n, (c, a, h) in enumerate(steps):
                        q = q_in[:, par, h, c] if isinstance(b, int) else q_in[:, bass.ds(par, 1), h, c].squeeze(1)
                        last = nc.tensor.matmul(s_ps[:, j % 2, QB * k:QB * (k + 1)], a[:, c, at], q,
                                                start=(n == 0), stop=(n == len(steps) - 1))
                last.then_inc(scores_ready, 1)

            def weigh(b, j):
                p = group(b, j)
                if p is None:
                    return
                chunk = 2 * b + j // CG
                par = (j // CG) % 2
                pe.wait_ge(lo_ready, p + 1)
                if j % CG == 0:
                    if started(chunk - 1):
                        pe.wait_ge(o_taken, chunk - 1)
                    for t in range(QT):
                        nc.tensor.matmul(o_ps[:, par, t, D + 2:D + 3], c_max[0:1, par, P * t:P * (t + 1)],
                                         one[0:1, 0:1], start=True, stop=True)
                for k in range(GK):
                    tile = GK * (j % GB) + k
                    for t in range(QT):
                        o = o_ps[:, par, t]
                        at = slice(QB * k + P * t, QB * k + P * (t + 1))
                        first = j % CG == 0 and k == 0
                        final = j % CG == CG - 1 and k == GK - 1
                        nc.tensor.matmul(o[:, 0:VW], p_hi[:, j % 2, at], v_hi[:, tile], start=first, stop=False)
                        nc.tensor.matmul(o[:, 0:D], p_hi[:, j % 2, at], v_lo[:, tile], start=False, stop=False)
                        last = nc.tensor.matmul(o[:, 0:VW], p_lo[:, j % 2, at], v_hi[:, tile], start=False, stop=final)
                last.then_inc(pv_done, 1)

            def body(b):
                for j in range(GB):
                    scores(b, j)
                    weigh(b, j - LAG_PV)

            bodies(pe, body, 2, NB)

        @block.vector
        def _(dve):
            def shift_scores(b, j):
                p = group(b, j)
                if p is None:
                    return
                if j % CG == 0:
                    dve.wait_ge(chunk_max, 2 * b + j // CG + 1)
                s = ring[:, j % GB].rearrange("p (k q) -> p k q", q=QB)
                m = c_max[:, (j // CG) % 2].unsqueeze(1).broadcast_to([P, GK, QB])
                nc.vector.tensor_tensor(s, s, m, ALU.subtract).then_inc(shifted, 1)

            def mask_scores(b, j):
                g = group(b, j)
                if g is None:
                    return
                m = j // 2
                dve.wait_ge(scores_ready, g + 1)
                dve.wait_ge(slot_filled, g + 1)
                dve.wait_ge(mask_loaded[m % 2], 16 * (2 * b + m // 2 + 1))
                held_apart(dve, b, dve_passed)
                nc.vector.copy_predicated(ring[:, j], mask_in[:, m % 2, GW * (j % 2):GW * (j % 2 + 1)],
                                          s_ps[:, j % 2]).then_inc(masked, 1)

            def running_max(b, j):
                g, at, done = group(b, j), j % CG, TOPS * (2 * b + j // CG)
                if g is None or at == 0:
                    return
                dve.wait_ge(masked, g + 1)
                if at == 1:
                    if started(done):
                        dve.wait_ge(top_steps, done)
                        dve.wait_ge(chunk_max, 2 * b + j // CG)
                    nc.vector.tensor_tensor(top[:], ring[:, j - 1], ring[:, j], ALU.max).then_inc(top_steps, 1)
                else:
                    dve.wait_ge(top_steps, done + at - 1)
                    nc.vector.tensor_tensor(top[:], top[:], ring[:, j], ALU.max).then_inc(top_steps, 1)

            def fold_max(b, j):
                g, at, done = group(b, j), j % CG, TOPS * (2 * b + j // CG)
                if g is not None and at == CG - 1:
                    dve.wait_ge(top_steps, done + 3)
                    nc.vector.tensor_tensor(top[:, 0:2 * QB], top[:, 0:2 * QB], top[:, 2 * QB:4 * QB],
                                            ALU.max).then_inc(top_steps, 1)
                    dve.wait_ge(top_steps, done + 4)
                    nc.vector.tensor_tensor(top[:, 0:QB], top[:, 0:QB], top[:, QB:2 * QB], ALU.max).then_inc(top_steps, 1)

            def low_parts(b, j):
                p = group(b, j)
                if p is None:
                    return
                dve.wait_ge(hi_ready, p + 1)
                if started(p - 1):
                    dve.wait_ge(pv_done, p - 1)
                nc.vector.tensor_tensor(p_lo[:, j % 2], ring[:, j % GB], p_hi[:, j % 2], ALU.subtract).then_inc(lo_ready, 1)

            def row_max(e):
                dve.wait_ge(o_taken, 2 * (e + 1))
                dve.wait_ge(e_loaded, 16 * (e + 1))
                if started(e):
                    dve.wait_ge(part_w_ready, QT * e)
                for c in range(2):
                    nc.vector.tensor_copy(tops[:, :, c:c + 1], o_in[:, c, :, D + 2:D + 3]).then_inc(negmax_steps, 1)
                nc.vector.tensor_copy(tops[:, :, 2:4], e_in[:, :, D:D + 2]).then_inc(negmax_steps, 1)
                dve.wait_ge(negmax_steps, NEG * e + 3)
                nc.vector.tensor_reduce(neg_max[:], tops[:], AX, ALU.max, negate=True).then_inc(negmax_steps, 1)

            def shares(e):
                dve.wait_ge(part_w_ready, QT * (e + 1))
                dve.wait_ge(sums_ready, 2 * (e + 1))
                nc.vector.tensor_tensor(prod[:], part_w[:], part_sum[:], ALU.mult).then_inc(share_steps, 1)
                dve.wait_ge(share_steps, SHARE * e + 1)
                nc.vector.tensor_reduce(denom[:], prod[:], AX, ALU.add).then_inc(share_steps, 1)
                dve.wait_ge(share_steps, SHARE * e + 2)
                nc.vector.reciprocal(rden[:], denom[:]).then_inc(share_steps, 1)
                dve.wait_ge(share_steps, SHARE * e + 3)
                if started(e):
                    dve.wait_ge(scaled, 4 * QT * e)
                nc.vector.tensor_tensor(share[:], part_w[:], rden[:].unsqueeze(2).broadcast_to([P, QT, 4]),
                                        ALU.mult).then_inc(share_steps, 1)

            def merge(e):
                dve.wait_ge(summed, SUMS * (e + 1))
                dve.wait_ge(rows_loaded, 32 * (e + 1))
                nc.vector.tensor_tensor(o_in[:, 1, :, 0:D], o_in[:, 1, :, 0:D], mx_in[:], ALU.max).then_inc(merged, 1)

            def moments(e):
                dve.wait_ge(y_ready, e + 1)
                for t in range(QT):
                    nc.vector.bn_stats(stats[:, t], o_in[:, 1, t, 0:D]).then_inc(stat_steps, 1)
                dve.wait_ge(stat_steps, STAT * e + QT)
                if started(e):
                    dve.wait_ge(rstd_steps, 2 * e)
                    dve.wait_ge(shift_ready, e)
                    held_apart(dve, e, dve_passed)
                for t in range(QT):
                    nc.vector.bn_aggr(mean_var[:, t], stats[:, t]).then_inc(stat_steps, 1)

            def norm_shift(e):
                dve.wait_ge(stat_steps, STAT * (e + 1))
                dve.wait_ge(rstd_steps, 2 * (e + 1))
                if started(e):
                    dve.wait_ge(normed, QT * e)
                nc.vector.scalar_tensor_tensor(shift[:], mean_var[:, :, 0], -1.0, rstd[:], ALU.mult, ALU.mult).then_inc(shift_ready, 1)

            def body(b):
                one_back, two_back = ending(b, 1), ending(b, 2)
                for j in range(GB):
                    mask_scores(b, j)
                    low_parts(b, j - LAG_LOW)
                    running_max(b, j)
                    shift_scores(b, j - LAG_SHIFT)
                    fold_max(b, j)
                    if two_back is not None:
                        if j == 0:
                            shares(two_back)
                        if j == 3:
                            merge(two_back)
                        if j == 4:
                            moments(two_back)
                        if j == 5:
                            norm_shift(two_back)
                    if j == 7 and one_back is not None:
                        row_max(one_back)

            bodies(dve, body, 3, NB + 1)

        @block.scalar
        def _(act):
            def exponentials(b, j):
                p = group(b, j)
                if p is None:
                    return
                act.wait_ge(shifted, p + 1)
                nc.scalar.activation(ring[:, j % GB], ring[:, j % GB], ACT.Exp).then_inc(exp_done, 1)
                act.wait_ge(exp_done, p + 1)
                if started(p - 1):
                    act.wait_ge(pv_done, p - 1)
                nc.scalar.activation(p_hi[:, j % 2], ring[:, j % GB], ACT.Copy).then_inc(hi_ready, 1)

            def take_output(e, c):
                act.wait_ge(pv_done, CG * (2 * e + c + 1))
                if started(e) and c == 0:
                    act.wait_ge(summed, SUMS * e)
                if started(e) and c == 1:
                    act.wait_ge(normed, QT * e)
                nc.scalar.activation(o_in[:, c, :, 0:OW], o_ps[:, c, :, 0:OW], ACT.Copy).then_inc(o_taken, 1)

            def part_weights(e):
                act.wait_ge(negmax_steps, NEG * e + 4)
                if started(e):
                    act.wait_ge(share_steps, SHARE * e)
                for t in range(QT):
                    nc.scalar.activation(part_w[:, t], tops[:, t], ACT.Exp, bias=neg_max[:, t:t + 1]).then_inc(part_w_ready, 1)

            def scale_parts(e):
                act.wait_ge(share_steps, SHARE * (e + 1))
                if started(e):
                    act.wait_ge(y_stored, 16 * e)
                for t in range(QT):
                    own = (o_in[:, 0, t, 0:D], o_in[:, 1, t, 0:D], e_in[:, t, 0:D])
                    for n, (part, to) in enumerate([(a, a) for a in own] + [(g_val[:], y_out[:, t])]):
                        nc.scalar.activation(to, part, ACT.Copy, scale=share[:, t, n:n + 1]).then_inc(scaled, 1)

            def normalise(e):
                act.wait_ge(shift_ready, e + 1)
                for t in range(QT):
                    nc.scalar.activation(y_out[:, t], o_in[:, 1, t, 0:D], ACT.Identity, bias=shift[:, t:t + 1],
                                         scale=rstd[:, t:t + 1]).then_inc(normed, 1)

            def body(b):
                one_back, two_back = ending(b, 1), ending(b, 2)
                for j in range(GB):
                    if two_back is not None:
                        if j == 0:
                            part_weights(two_back)
                        if j == 1:
                            scale_parts(two_back)
                        if j == 6:
                            normalise(two_back)
                    if one_back is not None:
                        if j == 5:
                            take_output(one_back, 0)
                        if j == 7:
                            take_output(one_back, 1)
                    exponentials(b, j - LAG_SHIFT)

            bodies(act, body, 3, NB + 1)

        @block.gpsimd
        def _(pool):
            def fill(slot):
                nc.gpsimd.memset(ring[:, slot], MASKED).then_inc(slot_filled, 1)

            def refill(b, j):
                p = group(b, j)
                if p is None or (isinstance(b, int) and p + GB >= NG):
                    return
                pool.wait_ge(lo_ready, p + 1)
                held_apart(pool, p, pool_passed)
                fill(j % GB)

            def all_max(b, j):
                g = group(b, j)
                if g is None:
                    return
                chunk, par = 2 * b + j // CG, j // CG
                pool.wait_ge(top_steps, TOPS * (chunk + 1))
                if started(chunk - 1):
                    pool.wait_ge(shifted, CG * (chunk - 1))
                    pool.wait_ge(pv_done, CG * (chunk - 2) + 1)
                    held_apart(pool, chunk, pool_passed)
                nc.gpsimd.partition_all_reduce(c_max[:, par], top[:, 0:QB], P, RMAX).then_inc(chunk_max, 1)

            def part_sums(e):
                pool.wait_ge(o_taken, 2 * (e + 1))
                if started(e):
                    pool.wait_ge(share_steps, SHARE * e)
                for c in range(2):
                    nc.gpsimd.tensor_tensor(part_sum[:, :, c:c + 1], o_in[:, c, :, D:D + 1], consts[:, 2:4].unsqueeze(2),
                                            ALU.mult).then_inc(sums_ready, 1)

            def sum_parts(e):
                pool.wait_ge(scaled, 4 * QT * (e + 1))
                nc.gpsimd.tensor_tensor(o_in[:, 1, :, 0:D], o_in[:, 1, :, 0:D], o_in[:, 0, :, 0:D], ALU.add).then_inc(summed, 1)
                pool.wait_ge(summed, SUMS * e + 1)
                nc.gpsimd.tensor_tensor(o_in[:, 1, :, 0:D], o_in[:, 1, :, 0:D], e_in[:, :, 0:D], ALU.add).then_inc(summed, 1)
                pool.wait_ge(summed, SUMS * e + 2)
                nc.gpsimd.tensor_tensor(o_in[:, 1, :, 0:D], o_in[:, 1, :, 0:D], y_out[:], ALU.add).then_inc(summed, 1)

            def add_x(e):
                pool.wait_ge(merged, e + 1)
                nc.gpsimd.tensor_tensor(o_in[:, 1, :, 0:D], o_in[:, 1, :, 0:D], x_in[:], ALU.add).then_inc(y_ready, 1)

            def inverse_std(e):
                pool.wait_ge(stat_steps, STAT * (e + 1))
                if started(e):
                    pool.wait_ge(normed, QT * e)
                    held_apart(pool, e, pool_passed)
                nc.gpsimd.tensor_scalar(var_eps[:], mean_var[:, :, 1], EPS, 1.0, ALU.add, ALU.mult).then_inc(rstd_steps, 1)
                pool.wait_ge(rstd_steps, 2 * e + 1)
                nc.gpsimd.tensor_tensor(rstd[:], var_eps[:], consts[:, 0:2], ALU.pow).then_inc(rstd_steps, 1)

            nc.gpsimd.memset(part_sum[:], 1.0).then_inc(pool_passed, 1)
            pool.wait_ge(pool_passed, 1)
            for slot in range(GB):
                fill(slot)

            def body(b):
                one_back, two_back = ending(b, 1), ending(b, 2)
                for j in range(GB):
                    if two_back is not None:
                        if j == 2:
                            sum_parts(two_back)
                        if j == 4:
                            add_x(two_back)
                        if j == 5:
                            inverse_std(two_back)
                    refill(b, j - LAG_LOW)
                    if j % CG == CG - 1:
                        all_max(b, j)
                    if j == 7 and one_back is not None:
                        part_sums(one_back)

            bodies(pool, body, 3, NB + 1)


def kernel(**inputs):
    import numpy as np
    import concourse.bacc as bacc
    from concourse.bass_utils import run_bass_kernel_spmd

    nc = bacc.Bacc("TRN2", target_bir_lowering=False, num_devices=1)
    arrays = {}

    def given(name, a):
        a = np.ascontiguousarray(a)
        arrays["in_" + name] = a
        return nc.dram_tensor("in_" + name, a.shape, mybir.dt.from_np(a.dtype), kind="ExternalInput").ap()

    x = np.asarray(inputs["x"])
    mx = np.asarray(inputs["L0_gnn_masked_x"])
    adj = np.asarray(inputs["adj"])
    mask = adj.T.reshape(GB // 2, 2 * GK, P, NB, QB).transpose(3, 0, 2, 1, 4).reshape(NB, GB // 2, P, 2 * GW)
    w = {}
    for name in ("Wlv", "blv", "Wgk", "Wgv", "bgv", "Wes", "Wev", "bev"):
        w[name] = given(name, np.asarray(inputs["L0_gnn_" + name]))
    for name in ("Wlq", "Wlk", "Wgq"):
        w[name + "T"] = given(name + "T", np.asarray(inputs["L0_gnn_" + name]).T)
    args = [given("x", x), given("xT", x.T), given("mxT", mx.T), given("mx", mx), given("mask", mask)]
    out = nc.dram_tensor("result", (N, D), FP32, kind="ExternalOutput").ap()
    build(nc, *args, w, out)
    r = run_bass_kernel_spmd(nc, [arrays], core_ids=[0])
    return r.results[0]["result"]
```

```python
import concourse.bass as bass
from concourse import mybir
from concourse.alu_op_type import AluOpType as ALU
from contextlib import ExitStack

FP32 = mybir.dt.float32
F32R = mybir.dt.float32r
U8 = mybir.dt.uint8
ACT = mybir.ActivationFunctionType
AX = mybir.AxisListType.X
RMAX = bass.bass_isa.ReduceOp.max

P = 128
N = 4096
D = 256
DC = D // P
KT = N // P
QB = 256
NB = N // QB
QT = QB // P
GK = 4
GW = GK * QB
GB = KT // GK
CG = GB // 2
NG = NB * GB
VW = D + 2
EW = D + 2
OW = D + 3
LAG_SHIFT = 5
LAG_LOW = 6
LAG_PV = 7
LW = 512
NL = N // LW
SCALE = 1.0 / 16.0
MASKED = -1e9
EPS = 1e-5


def started(v):
    return not isinstance(v, int) or v > 0


def held_apart(eng, count, passed):
    if not isinstance(count, int):
        eng.sem_inc(passed, 1)


def build(nc, x, xT, mxT, mx, mask, w, out):
    ctx = ExitStack()
    with ctx:
        def sb(name, shape, dt, to=ctx):
            return to.enter_context(nc.sbuf_tensor(name, shape, dt))

        def pb(name, shape, to=ctx):
            return to.enter_context(nc.psum_tensor(name, shape, FP32))

        def sem(name):
            return ctx.enter_context(nc.semaphore(name))

        q_dram = nc.dram_tensor("queries", (NB, P, DC, QB), FP32, kind="Internal").ap()
        e_dram = nc.dram_tensor("self_values", (NB, P, QT, EW), FP32, kind="Internal").ap()

        k_hi = sb("k_hi", [P, DC, N], F32R)
        k_lo = sb("k_lo", [P, DC, N], F32R)
        v_hi = sb("v_hi", [P, KT, VW], F32R)
        v_lo = sb("v_lo", [P, KT, D], F32R)
        g_val = sb("g_val", [P, D], FP32)
        one = sb("one", [P, 4], FP32)
        consts = sb("consts", [P, 4], FP32)

        prologue(nc, sb, pb, sem, xT, mxT, w, q_dram, e_dram, k_hi, k_lo, v_hi, v_lo, g_val, one, consts)
        attention(nc, sb, pb, sem, x, mx, mask, out, q_dram, e_dram, k_hi, k_lo, v_hi, v_lo, g_val, one, consts)


def prologue(nc, sb, pb, sem, xT, mxT, w, q_dram, e_dram, k_hi, k_lo, v_hi, v_lo, g_val, one, consts):
    XS = 4
    own = ExitStack()
    with own:
        stage = sb("stage", [P, XS, DC, LW], FP32, own)
        m_hi = sb("m_hi", [P, 2, DC, LW], F32R, own)
        m_lo = sb("m_lo", [P, 2, DC, LW], F32R, own)
        wlq = sb("wlqT", [P, DC, D], FP32, own)
        wlk = sb("wlkT", [P, DC, D], FP32, own)
        wgq = sb("wgqT", [P, DC, D], FP32, own)
        wgk = sb("wgk", [P, DC, D], FP32, own)
        wgv = sb("wgv", [P, DC, D], FP32, own)
        wlv = sb("wlv", [P, DC, D], FP32, own)
        wlv_hi = sb("wlv_hi", [P, DC, D], F32R, own)
        wlv_lo = sb("wlv_lo", [P, DC, D], F32R, own)
        wev = sb("wev", [P, DC, EW], FP32, own)
        wev_hi = sb("wev_hi", [P, DC, EW], F32R, own)
        wev_lo = sb("wev_lo", [P, DC, EW], F32R, own)
        mm_hi = sb("mm_hi", [P, DC, D], F32R, own)
        mm_lo = sb("mm_lo", [P, DC, D], F32R, own)
        blv = sb("blv", [P, D], FP32, own)
        bev = sb("bev", [P, EW], FP32, own)
        bgv = sb("bgv", [P, D], FP32, own)
        v_raw = sb("v_raw", [P, 2, 2, D], FP32, own)
        q_out = sb("q_out", [P, DC, LW], FP32, own)
        e_out = sb("e_out", [P, LW // P, EW], FP32, own)
        x_sum = sb("x_sum", [P, DC, NL], FP32, own)
        x_bar = sb("x_bar", [P, DC], FP32, own)
        x_wide = sb("x_wide", [P, DC, P], FP32, own)
        g_key = sb("g_key", [P, DC], FP32, own)

        m_ps = pb("m_ps", [P, DC, D], own)
        v_ps = pb("v_ps", [P, 2, 2, D], own)
        q_ps = pb("q_ps", [P, DC, LW], own)
        e_ps = pb("e_ps", [P, 2, 512], own)
        g_ps = pb("g_ps", [P, 512], own)

        wlv_in, blv_in = sem("wlv_in"), sem("blv_in")
        lqk_in, global_in, self_in = sem("lqk_in"), sem("global_in"), sem("self_in")
        LB = LW // QB
        x_staged = [sem(f"x_staged_{n}") for n in range(XS)]
        m_staged = [sem("m_staged_even"), sem("m_staged_odd")]
        tidy = sem("tidy")
        wlv_split, wev_split = sem("wlv_split"), sem("wev_split")
        mm_made, mm_hi_done, mm_split = sem("mm_made"), sem("mm_hi_done"), sem("mm_split")
        key_hi, key_lo = sem("key_hi"), sem("key_lo")
        v_made, v_added, v_hi_done, v_lo_done = sem("v_made"), sem("v_added"), sem("v_hi_done"), sem("v_lo_done")
        mean_made, g_key_made, g_key_in, g_score_made = sem("mean_made"), sem("g_key_made"), sem("g_key_in"), sem("g_score_made")
        g_score_in, g_val_made, g_val_done = sem("g_score_in"), sem("g_val_made"), sem("g_val_done")
        m_hi_done, m_lo_done = sem("m_hi_done"), sem("m_lo_done")
        q_made, q_taken = sem("q_made"), sem("q_taken")
        e_made, e_done = sem("e_made"), sem("e_done")
        q_stored = [sem(f"q_stored_half_{n}") for n in range(DC)]
        e_stored = [sem(f"e_stored_half_{n}") for n in range(LB)]
        sp_aside = sem("sp_aside")
        VP = LW // P // 2
        VT = KT // 2
        LT = LW // P
        HL = NL // 2

        def pieces(eng, body):
            body(0, 0)
            body(1, 1)
            with eng.Fori(1, HL) as u:
                body(2 * u, 0)
                body(2 * u + 1, 1)

        def inner(i):
            return not isinstance(i, int) or i >= 0

        block = own.enter_context(nc.Block())

        @block.sync
        def _(sp):
            xs = xT.rearrange("(c p) (l n) -> p l c n", p=P, n=LW)
            ms = mxT.rearrange("(c p) (l n) -> p l c n", p=P, n=LW)

            for i in range(NL):
                if i >= XS:
                    sp.wait_ge(key_lo, DC * (i - XS + 1))
                sp.dma_start(stage[:, i % XS], xs[:, i]).then_inc(x_staged[i % XS], 16)

            def load_m(i, h):
                if inner(i - 2):
                    sp.wait_ge(m_lo_done, i - 1)
                    held_apart(sp, i, sp_aside)
                else:
                    sp.wait_ge(key_lo, DC * (NL - XS + h + 1))
                sp.dma_start(stage[:, h], ms[:, bass.ds(i, 1)].squeeze(1)).then_inc(m_staged[h], 16)

            def store_q(i):
                for c in range(DC):
                    sp.wait_ge(q_taken, DC * i + c + 1)
                    held_apart(sp, i, sp_aside)
                    sp.dma_start(q_dram[bass.ds(LB * i, LB), :, c].rearrange("b p n -> p b n"),
                                 q_out[:, c].rearrange("p (b n) -> p b n", n=QB)).then_inc(q_stored[c], 16)

            load_m(0, 0)
            load_m(1, 1)
            with sp.Fori(1, HL) as u:
                for h in range(2):
                    load_m(2 * u + h, h)
                    store_q(2 * u - 2 + h)
            for i in range(NL - 2, NL):
                store_q(i)
            for c in range(DC):
                sp.wait_ge(q_stored[c], 16 * NL)

        @block.scalar
        def _(act):
            rows = "(c p) n -> p c n"

            def wide(name):
                return w[name].rearrange("(a n) -> a n", a=1).broadcast_to([P, D])

            act.dma_start(wlv[:], w["Wlv"].rearrange(rows, p=P)).then_inc(wlv_in, 16)
            act.dma_start(blv[:], wide("blv")).then_inc(blv_in, 16)
            act.wait_ge(wlv_in, 16)
            nc.scalar.activation(wlv_hi[:], wlv[:], ACT.Copy).then_inc(wlv_split, 1)

            def keys_high(i):
                act.wait_ge(x_staged[i % XS], 16 * (i // XS + 1))
                for c in range(DC):
                    nc.scalar.activation(k_hi[:, c, LW * i:LW * (i + 1)], stage[:, i % XS, c], ACT.Copy,
                                         accum_out=x_sum[:, c, i:i + 1]).then_inc(key_hi, 1)

            def values_high(i):
                for n in range(VP):
                    t = VP * i + n
                    act.wait_ge(v_added, t + 1)
                    nc.scalar.activation(v_hi[:, 2 * t:2 * t + 2, 0:D], v_raw[:, n], ACT.Copy).then_inc(v_hi_done, 1)

            for i in range(NL):
                keys_high(i)
                if i:
                    values_high(i - 1)
                if i == 1:
                    for name, to in (("WlqT", wlq), ("WlkT", wlk)):
                        act.dma_start(to[:], w[name].rearrange(rows, p=P)).then_inc(lqk_in, 16)
                if i == 2:
                    for name, to in (("Wgk", wgk), ("WgqT", wgq), ("Wgv", wgv)):
                        act.dma_start(to[:], w[name].rearrange(rows, p=P)).then_inc(global_in, 16)
                    act.dma_start(bgv[:], wide("bgv")).then_inc(global_in, 16)
                if i == 3:
                    act.dma_start(wev[:, :, 0:D], w["Wev"].rearrange(rows, p=P)).then_inc(self_in, 16)
                    act.dma_start(wev[:, 0, D:D + 1], w["Wes"][0:P, :]).then_inc(self_in, 16)
                    act.dma_start(wev[:, 1, D:D + 1], w["Wes"][P:D, :]).then_inc(self_in, 16)
                    act.dma_start(bev[:, 0:D], wide("bev")).then_inc(self_in, 16)
            act.wait_ge(mm_made, 1)
            nc.scalar.activation(mm_hi[:], m_ps[:], ACT.Copy, scale=SCALE).then_inc(mm_hi_done, 1)

            def rows_high(i, h):
                act.wait_ge(m_staged[h], 8 * (i - h) + 16)
                if inner(i - 2):
                    act.wait_ge(e_made, LT * (i - 1))
                nc.scalar.activation(m_hi[:, h], stage[:, h], ACT.Copy).then_inc(m_hi_done, 1)

            def take_queries(i, c):
                act.wait_ge(q_made, DC * i + c + 1)
                if inner(i - 1):
                    act.wait_ge(q_stored[c], 16 * i)
                nc.scalar.activation(q_out[:, c], q_ps[:, c], ACT.Copy).then_inc(q_taken, 1)

            rows_high(0, 0)
            values_high(NL - 1)
            act.wait_ge(g_score_in, 1)
            act.wait_ge(self_in, 64)
            nc.scalar.activation(wev_hi[:], wev[:], ACT.Copy).then_inc(wev_split, 1)
            for c in range(DC):
                take_queries(0, c)
            rows_high(1, 1)
            with act.Fori(1, HL) as u:
                for h in range(2):
                    i = 2 * u + h
                    for c in range(DC):
                        take_queries(i - 1, c)
                        if c == 0:
                            rows_high(i, h)
            for c in range(DC):
                take_queries(NL - 1, c)

        @block.gpsimd
        def _(pool):
            nc.gpsimd.memset(one[:], 1.0).then_inc(tidy, 1)
            nc.gpsimd.memset(consts[:, 0:2], -0.5).then_inc(tidy, 1)
            nc.gpsimd.memset(consts[:, 2:4], 1.0).then_inc(tidy, 1)
            nc.gpsimd.memset(bev[:, D:EW], 0.0).then_inc(tidy, 1)

            for i in range(NL):
                for c in range(DC):
                    pool.wait_ge(key_hi, DC * i + c + 1)
                    at = slice(LW * i, LW * (i + 1))
                    nc.gpsimd.tensor_tensor(k_lo[:, c, at], stage[:, i % XS, c], k_hi[:, c, at], ALU.subtract).then_inc(key_lo, 1)

            def store_e(i, h):
                for b in range(LB):
                    pool.wait_ge(e_done, LT * i + QT * (b + 1))
                    pool.dma_start(e_dram[bass.ds(i * LB + b, 1)].squeeze(0), e_out[:, QT * b:QT * (b + 1)]).then_inc(e_stored[b], 16)
            pieces(pool, store_e)
            for b in range(LB):
                pool.wait_ge(e_stored[b], 16 * NL)

        @block.vector
        def _(dve):
            dve.wait_ge(tidy, 4)
            nc.vector.tensor_copy(v_hi[:, :, D:VW], one[:, 0:2].unsqueeze(1).broadcast_to([P, KT, 2])).then_inc(tidy, 1)
            dve.wait_ge(wlv_in, 16)
            dve.wait_ge(wlv_split, 1)
            nc.vector.tensor_tensor(wlv_lo[:], wlv[:], wlv_hi[:], ALU.subtract).then_inc(wlv_split, 1)

            def add_bias(t, n):
                dve.wait_ge(v_made, t + 1)
                if inner(t - VP):
                    dve.wait_ge(v_hi_done, t - VP + 1)
                    dve.wait_ge(v_lo_done, t - VP + 1)
                nc.vector.tensor_tensor(v_raw[:, n], v_ps[:, n], blv[:].unsqueeze(1).broadcast_to([P, 2, D]),
                                        ALU.add).then_inc(v_added, 1)

            def values_low(t, n):
                dve.wait_ge(v_added, t + 1)
                dve.wait_ge(v_hi_done, t + 1)
                at = slice(2 * t, 2 * t + 2)
                nc.vector.tensor_tensor(v_lo[:, at], v_raw[:, n], v_hi[:, at, 0:D], ALU.subtract).then_inc(v_lo_done, 1)

            def body(i):
                for n in range(VP):
                    t = VP * i + n
                    add_bias(t, n)
                    if inner(t - 1):
                        values_low(t - 1, (n - 1) % VP)

            def rows_low(i, h):
                dve.wait_ge(m_hi_done, i + 1)
                if inner(i - 2):
                    dve.wait_ge(e_made, LT * (i - 1))
                nc.vector.tensor_tensor(m_lo[:, h], stage[:, h], m_hi[:, h], ALU.subtract).then_inc(m_lo_done, 1)

            dve.wait_ge(blv_in, 16)
            for i in range(NL - 1):
                body(i)
            dve.wait_ge(key_hi, DC * NL)
            nc.vector.tensor_reduce(x_bar[:], x_sum[:], AX, ALU.add).then_inc(mean_made, 1)
            dve.wait_ge(mean_made, 1)
            nc.vector.tensor_scalar(x_bar[:], x_bar[:], 1.0 / N, None, ALU.mult).then_inc(mean_made, 1)
            dve.wait_ge(mean_made, 2)
            nc.vector.tensor_copy(x_wide[:], x_bar[:].unsqueeze(2).broadcast_to([P, DC, P])).then_inc(mean_made, 1)
            dve.wait_ge(mm_hi_done, 1)
            nc.vector.scalar_tensor_tensor(mm_lo[:], m_ps[:], SCALE, mm_hi[:], ALU.mult, ALU.subtract).then_inc(mm_split, 1)
            add_bias(VT - 2, 0)
            values_low(VT - 3, 1)
            dve.wait_ge(g_key_made, 1)
            nc.vector.tensor_copy(g_key[:], g_ps[:, 0:DC]).then_inc(g_key_in, 1)
            add_bias(VT - 1, 1)
            values_low(VT - 2, 0)
            dve.wait_ge(g_score_made, 1)
            dve.wait_ge(self_in, 64)
            nc.vector.tensor_scalar(wev[:, :, D + 1:D + 2], g_ps[:, 2:2 + DC].unsqueeze(2), SCALE, None,
                                    ALU.mult).then_inc(g_score_in, 1)
            values_low(VT - 1, 1)
            rows_low(0, 0)
            dve.wait_ge(g_val_made, 1)
            dve.wait_ge(global_in, 64)
            nc.vector.tensor_tensor(g_val[:], g_ps[:, 16:16 + D], bgv[:], ALU.add).then_inc(g_val_done, 1)
            dve.wait_ge(wev_split, 1)
            dve.wait_ge(g_score_in, 1)
            nc.vector.tensor_tensor(wev_lo[:], wev[:], wev_hi[:], ALU.subtract).then_inc(wev_split, 1)

            def self_bias(i):
                for t in range(LT):
                    dve.wait_ge(e_made, LT * i + t + 1)
                    if inner(i - 1) and t % QT == 0:
                        dve.wait_ge(e_stored[t // QT], 16 * i)
                    nc.vector.tensor_tensor(e_out[:, t], e_ps[:, t % 2, 0:EW], bev[:], ALU.add).then_inc(e_done, 1)

            rows_low(1, 1)
            self_bias(0)
            with dve.Fori(1, HL) as u:
                for h in range(2):
                    rows_low(2 * u + h, h)
                    self_bias(2 * u + h - 1)
            self_bias(NL - 1)

        @block.tensor
        def _(pe):
            def product(out, hi, lo, rhs_hi, rhs_lo):
                steps = [(c, a, b) for c in range(DC) for a, b in ((hi, rhs_hi), (hi, rhs_lo), (lo, rhs_hi))]
                for n, (c, a, b) in enumerate(steps):
                    last = nc.tensor.matmul(out, a(c), b(c), start=(n == 0), stop=(n == len(steps) - 1))
                return last

            def values(i, n):
                t = VP * i + n
                if n == 0:
                    pe.wait_ge(key_lo, DC * (i + 1))
                if inner(t - 2):
                    pe.wait_ge(v_added, t - 1)
                for k in range(2):
                    at = slice((2 * t + k) * P, (2 * t + k + 1) * P)
                    last = product(v_ps[:, n, k], lambda c: k_hi[:, c, at], lambda c: k_lo[:, c, at],
                                   lambda c: wlv_hi[:, c], lambda c: wlv_lo[:, c])
                last.then_inc(v_made, 1)

            def body(i, h):
                for n in range(VP):
                    values(i, n)

            pe.wait_ge(wlv_split, 2)
            for i in range(NL - 2):
                body(i, i % 2)
            pe.wait_ge(lqk_in, 32)
            for i in range(DC):
                for c in range(DC):
                    last = nc.tensor.matmul(m_ps[:, i], wlq[:, c, P * i:P * (i + 1)], wlk[:, c],
                                            start=(c == 0), stop=(c == DC - 1))
            last.then_inc(mm_made, 1)
            body(NL - 2, 0)
            pe.wait_ge(mean_made, 2)
            pe.wait_ge(global_in, 64)
            for j in range(DC):
                for c in range(DC):
                    last = nc.tensor.matmul(g_ps[:, j:j + 1], wgk[:, c, P * j:P * (j + 1)], x_bar[:, c:c + 1],
                                            start=(c == 0), stop=(c == DC - 1))
            last.then_inc(g_key_made, 1)
            values(NL - 1, 0)
            pe.wait_ge(g_key_in, 1)
            for j in range(DC):
                for c in range(DC):
                    last = nc.tensor.matmul(g_ps[:, 2 + j:3 + j], wgq[:, c, P * j:P * (j + 1)], g_key[:, c:c + 1],
                                            start=(c == 0), stop=(c == DC - 1))
            last.then_inc(g_score_made, 1)
            values(NL - 1, 1)
            pe.wait_ge(mean_made, 3)
            pe.wait_ge(g_score_in, 1)
            for c in range(DC):
                last = nc.tensor.matmul(g_ps[:, 16:16 + D], x_wide[:, c], wgv[:, c], start=(c == 0), stop=(c == DC - 1))
            last.then_inc(g_val_made, 1)
            pe.wait_ge(mm_split, 1)

            def queries(i, h, j):
                if j == 0:
                    pe.wait_ge(m_hi_done, i + 1)
                    pe.wait_ge(m_lo_done, i + 1)
                if inner(i - 1):
                    pe.wait_ge(q_taken, DC * (i - 1) + j + 1)
                at = slice(P * j, P * (j + 1))
                product(q_ps[:, j], lambda c: mm_hi[:, c, at], lambda c: mm_lo[:, c, at],
                        lambda c: m_hi[:, h, c], lambda c: m_lo[:, h, c]).then_inc(q_made, 1)

            def self_values(i, h, t):
                at = slice(P * t, P * (t + 1))
                if inner(i - 1) or t >= 2:
                    pe.wait_ge(e_done, LT * i + t - 1)
                product(e_ps[:, t % 2, 0:EW], lambda c: m_hi[:, h, c, at], lambda c: m_lo[:, h, c, at],
                        lambda c: wev_hi[:, c], lambda c: wev_lo[:, c]).then_inc(e_made, 1)

            def body(i, h):
                for j in range(DC):
                    queries(i, h, j)
                    if not inner(i - 1) and j == 0:
                        pe.wait_ge(wev_split, 2)
                    for t in range(2 * j, 2 * j + 2):
                        self_values(i, h, t)
            pieces(pe, body)


def attention(nc, sb, pb, sem, x, mx, mask, out, q_dram, e_dram, k_hi, k_lo, v_hi, v_lo, g_val, one, consts):
    q_raw = sb("q_raw", [P, DC, QB], FP32)
    q_in = sb("q_in", [P, 2, 2, DC, QB], F32R)
    ring = sb("ring", [P, GB, GW], FP32)
    mask_in = sb("mask_in", [P, 2, 2 * GW], U8)
    p_hi = sb("p_hi", [P, 2, GW], F32R)
    p_lo = sb("p_lo", [P, 2, GW], F32R)
    top = sb("top", [P, GW], FP32)
    c_max = sb("c_max", [P, 2, QB], FP32)
    o_in = sb("o_in", [P, 2, QT, OW + 1], FP32)
    e_in = sb("e_in", [P, QT, EW], FP32)
    mx_in = sb("mx_in", [P, QT, D], FP32)
    y_rows = sb("y_rows", [P, QT, D], FP32)
    tops = sb("tops", [P, QT, 4], FP32)
    neg_max = sb("neg_max", [P, QT], FP32)
    part_w = sb("part_w", [P, QT, 4], FP32)
    part_sum = sb("part_sum", [P, QT, 4], FP32)
    prod = sb("prod", [P, QT, 4], FP32)
    denom = sb("denom", [P, QT], FP32)
    rden = sb("rden", [P, QT], FP32)
    share = sb("share", [P, QT, 4], FP32)
    stats = sb("stats", [P, QT, 6], FP32)
    mean_var = sb("mean_var", [P, QT, 2], FP32)
    var_eps = sb("var_eps", [P, QT], FP32)
    rstd = sb("rstd", [P, QT], FP32)
    shift = sb("shift", [P, QT], FP32)

    s_ps = pb("s_ps", [P, 2, GW])
    o_ps = pb("o_ps", [P, 2, QT, 512])

    q_hi_done, q_split = sem("q_hi_made"), sem("q_split")
    q_loaded, mask_loaded = sem("q_loaded"), [sem("mask_even"), sem("mask_odd")]
    mx_loaded, e_loaded, x_loaded, y_stored = sem("mx_loaded"), sem("e_loaded"), sem("x_loaded"), sem("y_stored")
    scores_ready, pv_done = sem("scores_ready"), sem("pv_done")
    slot_filled, chunk_max = sem("slot_filled"), sem("chunk_max")
    masked, top_steps, shifted, lo_ready = sem("masked"), sem("top_steps"), sem("shifted"), sem("lo_ready")
    exp_done, hi_ready = sem("exp_done"), sem("hi_ready")
    o_taken, part_w_ready, scaled, normed = sem("o_taken"), sem("part_w_ready"), sem("scaled"), sem("normed")
    negmax_steps, share_steps, merged, stat_steps, shift_ready = (
        sem("negmax_steps"), sem("share_steps"), sem("merged"), sem("stat_steps"), sem("shift_ready"))
    sums_ready = sem("sums_ready")
    summed, y_ready, rstd_steps = sem("summed"), sem("y_ready"), sem("rstd_steps")
    sp_passed, dve_passed, pool_passed = sem("sp_passed"), sem("dve_passed"), sem("pool_passed")
    TOPS = 5
    NEG, SHARE, STAT, SUMS = 4, 4, 4, 3

    def bodies(eng, body, first, last, end=NB):
        for b in range(first):
            body(b)
        with eng.Fori(first, end) as b:
            body(b)
        for b in range(end, last + 1):
            body(b)

    def group(b, j):
        g = b * GB + j
        return g if not isinstance(b, int) or 0 <= g < NG else None

    def ending(b, behind):
        return b - behind if not isinstance(b, int) or 0 <= b - behind < NB else None

    rows = "(b t p) d -> b p t d"
    x_rows, mx_rows, out_rows = (a.rearrange(rows, t=QT, p=P) for a in (x, mx, out))

    block = nc.Block()
    with block:
        @block.sync
        def _(sp):
            sp.dma_start(q_raw[:], q_dram[0]).then_inc(q_loaded, 16)

            def body(b):
                here, one_back, two_back, three_back = (ending(b, n) for n in range(4))

                def mask_piece(m):
                    if started(GB * b + 2 * m - 2):
                        sp.wait_ge(masked, GB * b + 2 * m - 2)
                        held_apart(sp, b, sp_passed)
                    sp.dma_start(mask_in[:, m % 2], mask[b, m]).then_inc(mask_loaded[m % 2], 16)

                if here is not None:
                    mask_piece(0)
                if three_back is not None:
                    sp.wait_ge(normed, QT * (three_back + 1))
                    sp.dma_start(out_rows[three_back], y_rows[:]).then_inc(y_stored, 16)
                if here is not None:
                    if not (isinstance(b, int) and b + 1 >= NB):
                        sp.wait_ge(q_split, b + 1)
                        held_apart(sp, b, sp_passed)
                        sp.dma_start(q_raw[:], q_dram[bass.ds(b + 1, 1)].squeeze(0)).then_inc(q_loaded, 16)
                    mask_piece(1)
                if two_back is not None:
                    if started(two_back):
                        sp.wait_ge(merged, two_back)
                    sp.dma_start(mx_in[:], mx_rows[two_back]).then_inc(mx_loaded, 16)
                if here is not None:
                    mask_piece(2)
                if two_back is not None:
                    sp.wait_ge(summed, SUMS * (two_back + 1))
                    sp.dma_start(y_rows[:], x_rows[two_back]).then_inc(x_loaded, 16)
                if one_back is not None:
                    if started(one_back):
                        sp.wait_ge(summed, SUMS * one_back)
                        held_apart(sp, b, sp_passed)
                        sp.wait_ge(e_loaded, 16 * one_back)
                    sp.dma_start(e_in[:], e_dram[one_back]).then_inc(e_loaded, 16)
                if here is not None:
                    mask_piece(3)
            bodies(sp, body, 3, NB + 2, NB - 1)
            sp.wait_ge(y_stored, 16 * NB)

        @block.tensor
        def _(pe):
            def scores(b, j):
                g = group(b, j)
                if g is None:
                    return
                if j == 0:
                    pe.wait_ge(q_split, b + 1)
                if started(g - 1):
                    pe.wait_ge(masked, g - 1)
                par = b % 2
                for k in range(GK):
                    tile = GK * j + k
                    at = slice(P * tile, P * (tile + 1))
                    steps = [(c, a, h) for c in range(DC) for a, h in ((k_hi, 0), (k_hi, 1), (k_lo, 0))]
                    for n, (c, a, h) in enumerate(steps):
                        q = q_in[:, par, h, c] if isinstance(b, int) else q_in[:, bass.ds(par, 1), h, c].squeeze(1)
                        last = nc.tensor.matmul(s_ps[:, j % 2, QB * k:QB * (k + 1)], a[:, c, at], q,
                                                start=(n == 0), stop=(n == len(steps) - 1))
                last.then_inc(scores_ready, 1)

            def weigh(b, j):
                p = group(b, j)
                if p is None:
                    return
                chunk = 2 * b + j // CG
                par = (j // CG) % 2
                pe.wait_ge(lo_ready, p + 1)
                if j % CG == 0:
                    if started(chunk - 1):
                        pe.wait_ge(o_taken, chunk - 1)
                    for t in range(QT):
                        nc.tensor.matmul(o_ps[:, par, t, D + 2:D + 3], c_max[0:1, par, P * t:P * (t + 1)],
                                         one[0:1, 0:1], start=True, stop=True)
                for k in range(GK):
                    tile = GK * (j % GB) + k
                    for t in range(QT):
                        o = o_ps[:, par, t]
                        at = slice(QB * k + P * t, QB * k + P * (t + 1))
                        first = j % CG == 0 and k == 0
                        final = j % CG == CG - 1 and k == GK - 1
                        nc.tensor.matmul(o[:, 0:VW], p_hi[:, j % 2, at], v_hi[:, tile], start=first, stop=False)
                        nc.tensor.matmul(o[:, 0:D], p_hi[:, j % 2, at], v_lo[:, tile], start=False, stop=False)
                        last = nc.tensor.matmul(o[:, 0:VW], p_lo[:, j % 2, at], v_hi[:, tile], start=False, stop=final)
                last.then_inc(pv_done, 1)

            def body(b):
                for j in range(GB):
                    scores(b, j)
                    weigh(b, j - LAG_PV)

            bodies(pe, body, 2, NB)

        @block.vector
        def _(dve):
            def shift_scores(b, j):
                p = group(b, j)
                if p is None:
                    return
                if j % CG == 0:
                    dve.wait_ge(chunk_max, 2 * b + j // CG + 1)
                s = ring[:, j % GB].rearrange("p (k q) -> p k q", q=QB)
                m = c_max[:, (j // CG) % 2].unsqueeze(1).broadcast_to([P, GK, QB])
                nc.vector.tensor_tensor(s, s, m, ALU.subtract).then_inc(shifted, 1)

            def mask_scores(b, j):
                g = group(b, j)
                if g is None:
                    return
                m = j // 2
                dve.wait_ge(scores_ready, g + 1)
                dve.wait_ge(slot_filled, g + 1)
                dve.wait_ge(mask_loaded[m % 2], 16 * (2 * b + m // 2 + 1))
                held_apart(dve, b, dve_passed)
                nc.vector.copy_predicated(ring[:, j], mask_in[:, m % 2, GW * (j % 2):GW * (j % 2 + 1)],
                                          s_ps[:, j % 2]).then_inc(masked, 1)

            def running_max(b, j):
                g, at, done = group(b, j), j % CG, TOPS * (2 * b + j // CG)
                if g is None or at == 0:
                    return
                dve.wait_ge(masked, g + 1)
                if at == 1:
                    if started(done):
                        dve.wait_ge(top_steps, done)
                        dve.wait_ge(chunk_max, 2 * b + j // CG)
                    nc.vector.tensor_tensor(top[:], ring[:, j - 1], ring[:, j], ALU.max).then_inc(top_steps, 1)
                else:
                    dve.wait_ge(top_steps, done + at - 1)
                    nc.vector.tensor_tensor(top[:], top[:], ring[:, j], ALU.max).then_inc(top_steps, 1)

            def fold_max(b, j):
                g, at, done = group(b, j), j % CG, TOPS * (2 * b + j // CG)
                if g is not None and at == CG - 1:
                    dve.wait_ge(top_steps, done + 3)
                    nc.vector.tensor_tensor(top[:, 0:2 * QB], top[:, 0:2 * QB], top[:, 2 * QB:4 * QB],
                                            ALU.max).then_inc(top_steps, 1)
                    dve.wait_ge(top_steps, done + 4)
                    nc.vector.tensor_tensor(top[:, 0:QB], top[:, 0:QB], top[:, QB:2 * QB], ALU.max).then_inc(top_steps, 1)

            def low_parts(b, j):
                p = group(b, j)
                if p is None:
                    return
                dve.wait_ge(hi_ready, p + 1)
                if started(p - 1):
                    dve.wait_ge(pv_done, p - 1)
                nc.vector.tensor_tensor(p_lo[:, j % 2], ring[:, j % GB], p_hi[:, j % 2], ALU.subtract).then_inc(lo_ready, 1)

            def row_max(e):
                dve.wait_ge(o_taken, 2 * (e + 1))
                dve.wait_ge(e_loaded, 16 * (e + 1))
                if started(e):
                    dve.wait_ge(part_w_ready, QT * e)
                for c in range(2):
                    nc.vector.tensor_copy(tops[:, :, c:c + 1], o_in[:, c, :, D + 2:D + 3]).then_inc(negmax_steps, 1)
                nc.vector.tensor_copy(tops[:, :, 2:4], e_in[:, :, D:D + 2]).then_inc(negmax_steps, 1)
                dve.wait_ge(negmax_steps, NEG * e + 3)
                nc.vector.tensor_reduce(neg_max[:], tops[:], AX, ALU.max, negate=True).then_inc(negmax_steps, 1)

            def shares(e):
                dve.wait_ge(part_w_ready, QT * (e + 1))
                dve.wait_ge(sums_ready, 2 * (e + 1))
                nc.vector.tensor_tensor(prod[:], part_w[:], part_sum[:], ALU.mult).then_inc(share_steps, 1)
                dve.wait_ge(share_steps, SHARE * e + 1)
                nc.vector.tensor_reduce(denom[:], prod[:], AX, ALU.add).then_inc(share_steps, 1)
                dve.wait_ge(share_steps, SHARE * e + 2)
                nc.vector.reciprocal(rden[:], denom[:]).then_inc(share_steps, 1)
                dve.wait_ge(share_steps, SHARE * e + 3)
                if started(e):
                    dve.wait_ge(scaled, 4 * QT * e)
                nc.vector.tensor_tensor(share[:], part_w[:], rden[:].unsqueeze(2).broadcast_to([P, QT, 4]),
                                        ALU.mult).then_inc(share_steps, 1)

            def merge(e):
                dve.wait_ge(summed, SUMS * (e + 1))
                dve.wait_ge(mx_loaded, 16 * (e + 1))
                nc.vector.tensor_tensor(o_in[:, 1, :, 0:D], o_in[:, 1, :, 0:D], mx_in[:], ALU.max).then_inc(merged, 1)

            def moments(e):
                dve.wait_ge(y_ready, e + 1)
                for t in range(QT):
                    nc.vector.bn_stats(stats[:, t], o_in[:, 1, t, 0:D]).then_inc(stat_steps, 1)
                dve.wait_ge(stat_steps, STAT * e + QT)
                if started(e):
                    dve.wait_ge(rstd_steps, 2 * e)
                    dve.wait_ge(shift_ready, e)
                    held_apart(dve, e, dve_passed)
                for t in range(QT):
                    nc.vector.bn_aggr(mean_var[:, t], stats[:, t]).then_inc(stat_steps, 1)

            def norm_shift(e):
                dve.wait_ge(stat_steps, STAT * (e + 1))
                dve.wait_ge(rstd_steps, 2 * (e + 1))
                if started(e):
                    dve.wait_ge(normed, QT * e)
                nc.vector.scalar_tensor_tensor(shift[:], mean_var[:, :, 0], -1.0, rstd[:], ALU.mult, ALU.mult).then_inc(shift_ready, 1)

            def body(b):
                one_back, two_back = ending(b, 1), ending(b, 2)
                for j in range(GB):
                    mask_scores(b, j)
                    shift_scores(b, j - LAG_SHIFT)
                    low_parts(b, j - LAG_LOW)
                    running_max(b, j)
                    fold_max(b, j)
                    if two_back is not None:
                        if j == 0:
                            shares(two_back)
                        if j == 3:
                            merge(two_back)
                        if j == 4:
                            moments(two_back)
                        if j == 5:
                            norm_shift(two_back)
                    if j == 7 and one_back is not None:
                        row_max(one_back)

            bodies(dve, body, 3, NB + 1)

        @block.scalar
        def _(act):
            def queries_high(b):
                act.wait_ge(q_loaded, 16 * (b + 1))
                if started(GB * (b - 1)):
                    act.wait_ge(scores_ready, GB * (b - 1))
                nc.scalar.activation(q_in[:, bass.ds(b % 2, 1), 0].squeeze(1), q_raw[:], ACT.Copy).then_inc(q_hi_done, 1)

            def exponentials(b, j):
                p = group(b, j)
                if p is None:
                    return
                act.wait_ge(shifted, p + 1)
                nc.scalar.activation(ring[:, j % GB], ring[:, j % GB], ACT.Exp).then_inc(exp_done, 1)
                act.wait_ge(exp_done, p + 1)
                if started(p - 1):
                    act.wait_ge(pv_done, p - 1)
                nc.scalar.activation(p_hi[:, j % 2], ring[:, j % GB], ACT.Copy).then_inc(hi_ready, 1)

            def take_output(e, c):
                act.wait_ge(pv_done, CG * (2 * e + c + 1))
                if started(e) and c == 0:
                    act.wait_ge(summed, SUMS * e)
                if started(e) and c == 1:
                    act.wait_ge(normed, QT * e)
                nc.scalar.activation(o_in[:, c, :, 0:OW], o_ps[:, c, :, 0:OW], ACT.Copy).then_inc(o_taken, 1)

            def part_weights(e):
                act.wait_ge(negmax_steps, NEG * e + 4)
                if started(e):
                    act.wait_ge(share_steps, SHARE * e)
                for t in range(QT):
                    nc.scalar.activation(part_w[:, t], tops[:, t], ACT.Exp, bias=neg_max[:, t:t + 1]).then_inc(part_w_ready, 1)

            def scale_parts(e):
                act.wait_ge(share_steps, SHARE * (e + 1))
                if started(e):
                    act.wait_ge(y_stored, 16 * e)
                for t in range(QT):
                    own = (o_in[:, 0, t, 0:D], o_in[:, 1, t, 0:D], e_in[:, t, 0:D])
                    for n, (part, to) in enumerate([(a, a) for a in own] + [(g_val[:], y_rows[:, t])]):
                        nc.scalar.activation(to, part, ACT.Copy, scale=share[:, t, n:n + 1]).then_inc(scaled, 1)

            def normalise(e):
                act.wait_ge(shift_ready, e + 1)
                for t in range(QT):
                    nc.scalar.activation(y_rows[:, t], o_in[:, 1, t, 0:D], ACT.Identity, bias=shift[:, t:t + 1],
                                         scale=rstd[:, t:t + 1]).then_inc(normed, 1)

            def body(b):
                one_back, two_back = ending(b, 1), ending(b, 2)
                for j in range(GB):
                    if two_back is not None:
                        if j == 0:
                            part_weights(two_back)
                        if j == 1:
                            scale_parts(two_back)
                        if j == 6:
                            normalise(two_back)
                    if one_back is not None:
                        if j == 5:
                            take_output(one_back, 0)
                        if j == 7:
                            take_output(one_back, 1)
                    if j == 2 and ending(b, -1) is not None:
                        queries_high(b + 1)
                    exponentials(b, j - LAG_SHIFT)

            queries_high(0)
            bodies(act, body, 3, NB + 1, NB - 1)

        @block.gpsimd
        def _(pool):
            def fill(slot):
                nc.gpsimd.memset(ring[:, slot], MASKED).then_inc(slot_filled, 1)

            def queries_low(b):
                pool.wait_ge(q_hi_done, b + 1)
                if started(GB * (b - 1)):
                    pool.wait_ge(scores_ready, GB * (b - 1))
                q = q_in[:, bass.ds(b % 2, 1)].squeeze(1)
                nc.gpsimd.tensor_tensor(q[:, 1], q_raw[:], q[:, 0], ALU.subtract).then_inc(q_split, 1)

            def refill(b, j):
                p = group(b, j)
                if p is None or (isinstance(b, int) and p + GB >= NG):
                    return
                pool.wait_ge(lo_ready, p + 1)
                held_apart(pool, p, pool_passed)
                fill(j % GB)

            def all_max(b, j):
                g = group(b, j)
                if g is None:
                    return
                chunk, par = 2 * b + j // CG, j // CG
                pool.wait_ge(top_steps, TOPS * (chunk + 1))
                if started(chunk - 1):
                    pool.wait_ge(shifted, CG * (chunk - 1))
                    pool.wait_ge(pv_done, CG * (chunk - 2) + 1)
                    held_apart(pool, chunk, pool_passed)
                nc.gpsimd.partition_all_reduce(c_max[:, par], top[:, 0:QB], P, RMAX).then_inc(chunk_max, 1)

            def part_sums(e):
                pool.wait_ge(o_taken, 2 * (e + 1))
                if started(e):
                    pool.wait_ge(share_steps, SHARE * e)
                for c in range(2):
                    nc.gpsimd.tensor_tensor(part_sum[:, :, c:c + 1], o_in[:, c, :, D:D + 1], consts[:, 2:4].unsqueeze(2),
                                            ALU.mult).then_inc(sums_ready, 1)

            def sum_parts(e):
                pool.wait_ge(scaled, 4 * QT * (e + 1))
                nc.gpsimd.tensor_tensor(o_in[:, 1, :, 0:D], o_in[:, 1, :, 0:D], o_in[:, 0, :, 0:D], ALU.add).then_inc(summed, 1)
                pool.wait_ge(summed, SUMS * e + 1)
                nc.gpsimd.tensor_tensor(o_in[:, 1, :, 0:D], o_in[:, 1, :, 0:D], e_in[:, :, 0:D], ALU.add).then_inc(summed, 1)
                pool.wait_ge(summed, SUMS * e + 2)
                nc.gpsimd.tensor_tensor(o_in[:, 1, :, 0:D], o_in[:, 1, :, 0:D], y_rows[:], ALU.add).then_inc(summed, 1)

            def add_x(e):
                pool.wait_ge(merged, e + 1)
                pool.wait_ge(x_loaded, 16 * (e + 1))
                nc.gpsimd.tensor_tensor(o_in[:, 1, :, 0:D], o_in[:, 1, :, 0:D], y_rows[:], ALU.add).then_inc(y_ready, 1)

            def inverse_std(e):
                pool.wait_ge(stat_steps, STAT * (e + 1))
                if started(e):
                    pool.wait_ge(normed, QT * e)
                    held_apart(pool, e, pool_passed)
                nc.gpsimd.tensor_scalar(var_eps[:], mean_var[:, :, 1], EPS, 1.0, ALU.add, ALU.mult).then_inc(rstd_steps, 1)
                pool.wait_ge(rstd_steps, 2 * e + 1)
                nc.gpsimd.tensor_tensor(rstd[:], var_eps[:], consts[:, 0:2], ALU.pow).then_inc(rstd_steps, 1)

            nc.gpsimd.memset(part_sum[:], 1.0).then_inc(pool_passed, 1)
            pool.wait_ge(pool_passed, 1)
            fill(0)
            queries_low(0)
            for slot in range(1, GB):
                fill(slot)

            def body(b):
                one_back, two_back = ending(b, 1), ending(b, 2)
                for j in range(GB):
                    if two_back is not None:
                        if j == 2:
                            sum_parts(two_back)
                        if j == 4:
                            add_x(two_back)
                        if j == 5:
                            inverse_std(two_back)
                    refill(b, j - LAG_LOW)
                    if j % CG == CG - 1:
                        all_max(b, j)
                    if j == 3 and ending(b, -1) is not None:
                        queries_low(b + 1)
                    if j == 7 and one_back is not None:
                        part_sums(one_back)

            bodies(pool, body, 3, NB + 1, NB - 1)


def kernel(**inputs):
    import numpy as np
    import concourse.bacc as bacc
    from concourse.bass_utils import run_bass_kernel_spmd

    nc = bacc.Bacc("TRN2", target_bir_lowering=False, num_devices=1)
    arrays = {}

    def given(name, a):
        a = np.ascontiguousarray(a)
        arrays["in_" + name] = a
        return nc.dram_tensor("in_" + name, a.shape, mybir.dt.from_np(a.dtype), kind="ExternalInput").ap()

    x = np.asarray(inputs["x"])
    mx = np.asarray(inputs["L0_gnn_masked_x"])
    adj = np.asarray(inputs["adj"])
    mask = adj.T.reshape(GB // 2, 2 * GK, P, NB, QB).transpose(3, 0, 2, 1, 4).reshape(NB, GB // 2, P, 2 * GW)
    w = {}
    for name in ("Wlv", "blv", "Wgk", "Wgv", "bgv", "Wes", "Wev", "bev"):
        w[name] = given(name, np.asarray(inputs["L0_gnn_" + name]))
    for name in ("Wlq", "Wlk", "Wgq"):
        w[name + "T"] = given(name + "T", np.asarray(inputs["L0_gnn_" + name]).T)
    args = [given("x", x), given("xT", x.T), given("mxT", mx.T), given("mx", mx), given("mask", mask)]
    out = nc.dram_tensor("result", (N, D), FP32, kind="ExternalOutput").ap()
    build(nc, *args, w, out)
    r = run_bass_kernel_spmd(nc, [arrays], core_ids=[0])
    return r.results[0]["result"]
```

```python
import concourse.bass as bass
from concourse import mybir
from concourse.alu_op_type import AluOpType as ALU
from contextlib import ExitStack

FP32 = mybir.dt.float32
F32R = mybir.dt.float32r
U8 = mybir.dt.uint8
ACT = mybir.ActivationFunctionType
AX = mybir.AxisListType.X
RMAX = bass.bass_isa.ReduceOp.max

P = 128
N = 4096
D = 256
DC = D // P
KT = N // P
QB = 256
NB = N // QB
QT = QB // P
GK = 4
GW = GK * QB
GB = KT // GK
CG = GB // 2
NG = NB * GB
VW = D + 2
EW = D + 2
OW = D + 3
LAG_SHIFT = 5
LAG_LOW = 6
LAG_PV = 7
LW = 512
NL = N // LW
SCALE = 1.0 / 16.0
MASKED = -1e9
EPS = 1e-5


def started(v):
    return not isinstance(v, int) or v > 0


def held_apart(eng, count, passed):
    if not isinstance(count, int):
        eng.sem_inc(passed, 1)


def build(nc, x, xT, mxT, mx, mask, w, out):
    ctx = ExitStack()
    with ctx:
        def sb(name, shape, dt, to=ctx):
            return to.enter_context(nc.sbuf_tensor(name, shape, dt))

        def pb(name, shape, to=ctx):
            return to.enter_context(nc.psum_tensor(name, shape, FP32))

        def sem(name):
            return ctx.enter_context(nc.semaphore(name))

        q_dram = nc.dram_tensor("queries", (NB, P, DC, QB), FP32, kind="Internal").ap()
        e_dram = nc.dram_tensor("self_values", (NB, P, QT, EW), FP32, kind="Internal").ap()

        k_hi = sb("k_hi", [P, DC, N], F32R)
        k_lo = sb("k_lo", [P, DC, N], F32R)
        v_hi = sb("v_hi", [P, KT, VW], F32R)
        v_lo = sb("v_lo", [P, KT, D], F32R)
        g_val = sb("g_val", [P, D], FP32)
        one = sb("one", [P, 4], FP32)
        consts = sb("consts", [P, 4], FP32)
        q_raw = sb("q_raw", [P, DC, QB], FP32)
        q_in = sb("q_in", [P, 2, 2, DC, QB], F32R)
        mask_in = sb("mask_in", [P, 2, 2 * GW], U8)
        q_loaded, q_hi_done, q_split = sem("q_loaded"), sem("q_hi_done"), sem("q_split")
        mask_loaded = [sem("mask_even"), sem("mask_odd")]

        last_stores = prologue(
            nc, sb, pb, sem, xT, mxT, w, mask, q_dram, e_dram, k_hi, k_lo, v_hi, v_lo, g_val, one, consts,
            q_raw, q_in, mask_in, q_loaded, q_hi_done, q_split, mask_loaded)
        attention(
            nc, sb, pb, sem, x, mx, mask, out, q_dram, e_dram, k_hi, k_lo, v_hi, v_lo, g_val, one, consts,
            q_raw, q_in, mask_in, q_loaded, q_hi_done, q_split, mask_loaded, last_stores)


def prologue(nc, sb, pb, sem, xT, mxT, w, mask, q_dram, e_dram, k_hi, k_lo, v_hi, v_lo, g_val, one, consts,
             q_raw, q_in, mask_in, q_loaded, q_hi_done, q_split, mask_loaded):
    WARM = 5
    XS = 4
    own = ExitStack()
    with own:
        stage = sb("stage", [P, XS, DC, LW], FP32, own)
        with ExitStack() as early:
            wlq, wlk, wgq, wgk, wgv, wlv = (sb(name, [P, DC, D], FP32, early)
                                            for name in ("wlqT", "wlkT", "wgqT", "wgk", "wgv", "wlv"))
        m_lo = [sb(name, [P, DC, LW], F32R, own) for name in ("m_lo_even", "m_lo_odd")]
        m_hi = [sb(name, [P, DC, LW], F32R, own) for name in ("m_hi_odd", "m_hi_even")][::-1]
        wlv_hi = sb("wlv_hi", [P, DC, D], F32R, own)
        wlv_lo = sb("wlv_lo", [P, DC, D], F32R, own)
        wev = sb("wev", [P, DC, EW], FP32, own)
        wev_hi = sb("wev_hi", [P, DC, EW], F32R, own)
        wev_lo = sb("wev_lo", [P, DC, EW], F32R, own)
        mm_hi = sb("mm_hi", [P, DC, D], F32R, own)
        mm_lo = sb("mm_lo", [P, DC, D], F32R, own)
        blv = sb("blv", [P, D], FP32, own)
        bev = sb("bev", [P, EW], FP32, own)
        bgv = sb("bgv", [P, D], FP32, own)
        v_raw = sb("v_raw", [P, 2, 2, D], FP32, own)
        x_sum = sb("x_sum", [P, DC, NL], FP32, own)
        x_bar = sb("x_bar", [P, DC], FP32, own)
        x_wide = sb("x_wide", [P, DC, P], FP32, own)
        g_key = sb("g_key", [P, DC], FP32, own)
        zeros = sb("zeros", [P, D], FP32, own)
        q_out = sb("q_out", [P, DC, LW], FP32, own)
        e_out = sb("e_out", [P, LW // P, EW], FP32, own)

        m_ps = pb("m_ps", [P, DC, D], own)
        v_ps = pb("v_ps", [P, 2, 2, D], own)
        q_ps = pb("q_ps", [P, DC, LW], own)
        e_ps = pb("e_ps", [P, 2, 512], own)
        g_ps = pb("g_ps", [P, 512], own)

        wlv_in, blv_in = sem("wlv_in"), sem("blv_in")
        lqk_in, global_in, self_in = sem("lqk_in"), sem("global_in"), sem("self_in")
        LB = LW // QB
        x_staged = [sem(f"x_staged_{n}") for n in range(XS)]
        m_staged = [sem("m_staged_even"), sem("m_staged_odd")]
        tidy = sem("tidy")
        wlv_split, wev_split = sem("wlv_split"), sem("wev_split")
        mm_made, mm_hi_done, mm_split = sem("mm_made"), sem("mm_hi_done"), sem("mm_split")
        key_hi, first_low, key_lo = sem("key_hi"), sem("first_low"), sem("key_lo")
        zeros_made = sem("zeros_made")
        v_made, v_added, v_hi_done, v_lo_done = sem("v_made"), sem("v_added"), sem("v_hi_done"), sem("v_lo_done")
        mean_made, g_key_made, g_key_in, g_score_made = sem("mean_made"), sem("g_key_made"), sem("g_key_in"), sem("g_score_made")
        g_score_in, g_val_made, g_val_done = sem("g_score_in"), sem("g_val_made"), sem("g_val_done")
        m_hi_done, m_lo_done = sem("m_hi_done"), sem("m_lo_done")
        q_made, q_taken = sem("q_made"), sem("q_taken")
        e_made, e_done = sem("e_made"), sem("e_done")
        q_stored = [sem(f"q_stored_half_{n}") for n in range(DC)]
        e_stored = [sem(f"e_stored_half_{n}") for n in range(LB)]
        sp_aside = sem("sp_aside")
        VP = LW // P // 2
        VT = KT // 2
        LT = LW // P
        HL = NL // 2

        def pieces(eng, body):
            body(0, 0)
            body(1, 1)
            with eng.Fori(1, HL) as u:
                body(2 * u, 0)
                body(2 * u + 1, 1)

        def inner(i):
            return not isinstance(i, int) or i >= 0

        block = own.enter_context(nc.Block())

        @block.sync
        def _(sp):
            rows = "(c p) n -> p c n"
            xs = xT.rearrange("(c p) (l n) -> p l c n", p=P, n=LW)
            ms = mxT.rearrange("(c p) (l n) -> p l c n", p=P, n=LW)

            def wide(name):
                return w[name].rearrange("(a n) -> a n", a=1).broadcast_to([P, D])

            def square(name):
                return w[name].rearrange(rows, p=P)

            weights = {0: [(blv[:], wide("blv"), blv_in)],
                       1: [(wlq[:], square("WlqT"), lqk_in), (wlk[:], square("WlkT"), lqk_in)],
                       3: [(wgk[:], square("Wgk"), global_in), (wgq[:], square("WgqT"), global_in)],
                       4: [(wgv[:], square("Wgv"), global_in), (wev[:, :, 0:D], square("Wev"), self_in)],
                       5: [(bgv[:], wide("bgv"), global_in), (wev[:, 0, D:D + 1], w["Wes"][0:P, :], self_in),
                           (wev[:, 1, D:D + 1], w["Wes"][P:D, :], self_in), (bev[:, 0:D], wide("bev"), self_in)]}
            for i in range(NL):
                if i == XS:
                    sp.wait_ge(first_low, DC)
                if i > XS:
                    sp.wait_ge(key_lo, DC * (i - XS))
                sp.dma_start(stage[:, i % XS], xs[:, i]).then_inc(x_staged[i % XS], 16)
                for to, array, done in weights.get(i, []):
                    sp.dma_start(to, array).then_inc(done, 16)

            def load_m(i, h):
                if inner(i - 2):
                    sp.wait_ge(m_lo_done, i - 1)
                    held_apart(sp, i, sp_aside)
                else:
                    sp.wait_ge(key_lo, DC * (NL - XS + h))
                sp.dma_start(stage[:, h], ms[:, bass.ds(i, 1)].squeeze(1)).then_inc(m_staged[h], 16)

            def store(i):
                for n in range(2):
                    sp.wait_ge(q_taken, DC * i + n + 1)
                    held_apart(sp, i, sp_aside)
                    sp.dma_start(q_dram[bass.ds(LB * i, LB), :, n].rearrange("b p n -> p b n"),
                                 q_out[:, n].rearrange("p (b n) -> p b n", n=QB)).then_inc(q_stored[n], 16)
                    sp.wait_ge(e_done, LT * i + QT * (n + 1))
                    held_apart(sp, i, sp_aside)
                    sp.dma_start(e_dram[bass.ds(LB * i + n, 1)].squeeze(0), e_out[:, QT * n:QT * (n + 1)]).then_inc(e_stored[n], 16)

            load_m(0, 0)
            load_m(1, 1)
            with sp.Fori(1, HL) as u:
                for h in range(2):
                    load_m(2 * u + h, h)
                    store(2 * u - 2 + h)
            for n in range(2):
                sp.wait_ge(q_stored[n], 16 * (NL - 2))
            sp.dma_start(q_raw[:], q_dram[0]).then_inc(q_loaded, 16)
            sp.dma_start(mask_in[:, 0], mask[0, 0]).then_inc(mask_loaded[0], 16)
            sp.dma_start(mask_in[:, 1], mask[0, 1]).then_inc(mask_loaded[1], 16)
            for i in range(NL - 2, NL):
                store(i)

        @block.scalar
        def _(act):
            rows = "(c p) n -> p c n"
            act.dma_start(wlv[:], w["Wlv"].rearrange(rows, p=P)).then_inc(wlv_in, 16)

            def keys_high(i):
                act.wait_ge(x_staged[i % XS], 16 * (i // XS + 1))
                for c in range(DC):
                    nc.scalar.activation(k_hi[:, c, LW * i:LW * (i + 1)], stage[:, i % XS, c], ACT.Copy,
                                         accum_out=x_sum[:, c, i:i + 1]).then_inc(key_hi, 1)

            def values_high(i):
                for n in range(VP):
                    t = VP * i + n
                    act.wait_ge(v_added, t + 1)
                    nc.scalar.activation(v_hi[:, 2 * t:2 * t + 2, 0:D], v_raw[:, n], ACT.Copy).then_inc(v_hi_done, 1)

            keys_high(0)
            act.wait_ge(wlv_in, 16)
            nc.scalar.activation(wlv_hi[:], wlv[:], ACT.Copy).then_inc(wlv_split, 1)
            for i in range(1, NL):
                keys_high(i)
                if i >= 2:
                    values_high(i - 2)
            values_high(NL - 2)
            act.wait_ge(mm_made, 1)
            nc.scalar.activation(mm_hi[:], m_ps[:], ACT.Copy, scale=SCALE).then_inc(mm_hi_done, 1)

            def rows_high(i, h):
                act.wait_ge(m_staged[h], 8 * (i - h) + 16)
                if inner(i - 2):
                    act.wait_ge(e_made, LT * (i - 1))
                nc.scalar.activation(m_hi[h][:], stage[:, h], ACT.Copy).then_inc(m_hi_done, 1)

            def take_queries(i, c, before=True):
                act.wait_ge(q_made, DC * i + c + 1)
                if before:
                    act.wait_ge(q_stored[c], 16 * i)
                nc.scalar.activation(q_out[:, c], q_ps[:, c], ACT.Copy).then_inc(q_taken, 1)

            rows_high(0, 0)
            values_high(NL - 1)
            act.wait_ge(g_score_in, 1)
            act.wait_ge(self_in, 64)
            nc.scalar.activation(wev_hi[:], wev[:], ACT.Copy).then_inc(wev_split, 1)
            act.wait_ge(g_val_made, 1)
            rows_high(1, 1)
            for i in range(2):
                for c in range(DC):
                    take_queries(i, c, i > 0)
                rows_high(i + 2, i)
            with act.Fori(1, HL - 1) as u:
                for h in range(2):
                    for c in range(DC):
                        take_queries(2 * u + h, c)
                    rows_high(2 * u + 2 + h, h)
            for c in range(DC):
                take_queries(NL - 2, c)
            act.wait_ge(q_loaded, 16)
            nc.scalar.activation(q_in[:, 0, 0], q_raw[:], ACT.Copy).then_inc(q_hi_done, 1)
            for c in range(DC):
                take_queries(NL - 1, c)

        @block.gpsimd
        def _(pool):
            nc.gpsimd.memset(one[:], 1.0).then_inc(tidy, 1)
            nc.gpsimd.memset(consts[:, 0:2], -0.5).then_inc(tidy, 1)
            nc.gpsimd.memset(consts[:, 2:4], 1.0).then_inc(tidy, 1)
            nc.gpsimd.memset(bev[:, D:EW], 0.0).then_inc(tidy, 1)

            for i in range(1, NL):
                for c in range(DC):
                    pool.wait_ge(key_hi, DC * i + c + 1)
                    at = slice(LW * i, LW * (i + 1))
                    nc.gpsimd.tensor_tensor(k_lo[:, c, at], stage[:, i % XS, c], k_hi[:, c, at], ALU.subtract).then_inc(key_lo, 1)

        @block.vector
        def _(dve):
            nc.vector.memset(zeros[:], 0.0).then_inc(zeros_made, 1)
            dve.wait_ge(tidy, 4)
            nc.vector.tensor_copy(v_hi[:, :, D:VW], one[:, 0:2].unsqueeze(1).broadcast_to([P, KT, 2])).then_inc(tidy, 1)
            for c in range(DC):
                dve.wait_ge(key_hi, c + 1)
                nc.vector.tensor_tensor(k_lo[:, c, 0:LW], stage[:, 0, c], k_hi[:, c, 0:LW], ALU.subtract).then_inc(first_low, 1)
            dve.wait_ge(wlv_in, 16)
            dve.wait_ge(wlv_split, 1)
            nc.vector.tensor_tensor(wlv_lo[:], wlv[:], wlv_hi[:], ALU.subtract).then_inc(wlv_split, 1)

            def add_bias(t, n):
                dve.wait_ge(v_made, t + 1)
                if inner(t - VP):
                    dve.wait_ge(v_hi_done, t - VP + 1)
                    dve.wait_ge(v_lo_done, t - VP + 1)
                nc.vector.tensor_tensor(v_raw[:, n], v_ps[:, n], blv[:].unsqueeze(1).broadcast_to([P, 2, D]),
                                        ALU.add).then_inc(v_added, 1)

            def values_low(t, n):
                dve.wait_ge(v_added, t + 1)
                dve.wait_ge(v_hi_done, t + 1)
                at = slice(2 * t, 2 * t + 2)
                nc.vector.tensor_tensor(v_lo[:, at], v_raw[:, n], v_hi[:, at, 0:D], ALU.subtract).then_inc(v_lo_done, 1)

            def piece_values(i):
                for n in range(VP):
                    t = VP * i + n
                    add_bias(t, n)
                    if inner(t - 1):
                        values_low(t - 1, (n - 1) % VP)

            def rows_low(i, h):
                dve.wait_ge(m_hi_done, i + 1)
                if inner(i - 2):
                    dve.wait_ge(e_made, LT * (i - 1))
                nc.vector.tensor_tensor(m_lo[h][:], stage[:, h], m_hi[h][:], ALU.subtract).then_inc(m_lo_done, 1)

            dve.wait_ge(blv_in, 16)
            for i in range(NL - 2):
                piece_values(i)
            dve.wait_ge(key_hi, DC * NL)
            nc.vector.tensor_reduce(x_bar[:], x_sum[:], AX, ALU.add).then_inc(mean_made, 1)
            dve.wait_ge(mean_made, 1)
            nc.vector.tensor_scalar(x_bar[:], x_bar[:], 1.0 / N, None, ALU.mult).then_inc(mean_made, 1)
            dve.wait_ge(mean_made, 2)
            nc.vector.tensor_copy(x_wide[:], x_bar[:].unsqueeze(2).broadcast_to([P, DC, P])).then_inc(mean_made, 1)
            piece_values(NL - 2)
            dve.wait_ge(mm_hi_done, 1)
            nc.vector.scalar_tensor_tensor(mm_lo[:], m_ps[:], SCALE, mm_hi[:], ALU.mult, ALU.subtract).then_inc(mm_split, 1)
            dve.wait_ge(g_key_made, 1)
            nc.vector.tensor_copy(g_key[:], g_ps[:, 0:DC]).then_inc(g_key_in, 1)
            add_bias(VT - 2, 0)
            values_low(VT - 3, 1)
            dve.wait_ge(g_score_made, 1)
            dve.wait_ge(self_in, 64)
            nc.vector.tensor_scalar(wev[:, :, D + 1:D + 2], g_ps[:, 2:2 + DC].unsqueeze(2), SCALE, None,
                                    ALU.mult).then_inc(g_score_in, 1)
            rows_low(0, 0)
            add_bias(VT - 1, 1)
            values_low(VT - 2, 0)
            dve.wait_ge(wev_split, 1)
            dve.wait_ge(g_score_in, 1)
            nc.vector.tensor_tensor(wev_lo[:], wev[:], wev_hi[:], ALU.subtract).then_inc(wev_split, 1)
            values_low(VT - 1, 1)
            dve.wait_ge(g_val_made, 1)
            dve.wait_ge(global_in, 64)
            nc.vector.tensor_tensor(g_val[:], g_ps[:, 16:16 + D], bgv[:], ALU.add).then_inc(g_val_done, 1)
            rows_low(1, 1)

            def self_bias(i, before=True):
                for t in range(LT):
                    dve.wait_ge(e_made, LT * i + t + 1)
                    if before and t % QT == 0:
                        dve.wait_ge(e_stored[t // QT], 16 * i)
                    nc.vector.tensor_tensor(e_out[:, t], e_ps[:, t % 2, 0:EW], bev[:], ALU.add).then_inc(e_done, 1)

            self_bias(0, False)
            rows_low(2, 0)
            self_bias(1)
            rows_low(3, 1)
            with dve.Fori(1, HL - 1) as u:
                for h in range(2):
                    self_bias(2 * u + h)
                    rows_low(2 * u + 2 + h, h)
            self_bias(NL - 2)
            dve.wait_ge(q_hi_done, 1)
            nc.vector.tensor_tensor(q_in[:, 0, 1], q_raw[:], q_in[:, 0, 0], ALU.subtract).then_inc(q_split, 1)
            self_bias(NL - 1)

        @block.tensor
        def _(pe):
            def product(out, hi, lo, rhs_hi, rhs_lo):
                steps = [(c, a, b) for c in range(DC) for a, b in ((hi, rhs_hi), (hi, rhs_lo), (lo, rhs_hi))]
                for n, (c, a, b) in enumerate(steps):
                    last = nc.tensor.matmul(out, a(c), b(c), start=(n == 0), stop=(n == len(steps) - 1))
                return last

            def values(i, n):
                t = VP * i + n
                if n == 0:
                    if i:
                        pe.wait_ge(key_lo, DC * i)
                    else:
                        pe.wait_ge(first_low, DC)
                if inner(t - 2):
                    pe.wait_ge(v_added, t - 1)
                for k in range(2):
                    at = slice((2 * t + k) * P, (2 * t + k + 1) * P)
                    last = product(v_ps[:, n, k], lambda c: k_hi[:, c, at], lambda c: k_lo[:, c, at],
                                   lambda c: wlv_hi[:, c], lambda c: wlv_lo[:, c])
                last.then_inc(v_made, 1)

            def piece_values(i):
                for n in range(VP):
                    values(i, n)

            pe.wait_ge(zeros_made, 1)
            for n in range(WARM):
                nc.tensor.matmul(g_ps[:, D:2 * D], zeros[:, 0:P], zeros[:], start=True, stop=True)
            pe.wait_ge(wlv_split, 2)
            for i in range(NL - 2):
                piece_values(i)
            pe.wait_ge(lqk_in, 32)
            for i in range(DC):
                for c in range(DC):
                    last = nc.tensor.matmul(m_ps[:, i], wlq[:, c, P * i:P * (i + 1)], wlk[:, c],
                                            start=(c == 0), stop=(c == DC - 1))
            last.then_inc(mm_made, 1)
            piece_values(NL - 2)
            pe.wait_ge(mean_made, 2)
            pe.wait_ge(global_in, 64)
            for j in range(DC):
                for c in range(DC):
                    last = nc.tensor.matmul(g_ps[:, j:j + 1], wgk[:, c, P * j:P * (j + 1)], x_bar[:, c:c + 1],
                                            start=(c == 0), stop=(c == DC - 1))
            last.then_inc(g_key_made, 1)
            values(NL - 1, 0)
            pe.wait_ge(g_key_in, 1)
            for j in range(DC):
                for c in range(DC):
                    last = nc.tensor.matmul(g_ps[:, 2 + j:3 + j], wgq[:, c, P * j:P * (j + 1)], g_key[:, c:c + 1],
                                            start=(c == 0), stop=(c == DC - 1))
            last.then_inc(g_score_made, 1)
            values(NL - 1, 1)
            pe.wait_ge(mean_made, 3)
            pe.wait_ge(g_score_in, 1)
            for c in range(DC):
                last = nc.tensor.matmul(g_ps[:, 16:16 + D], x_wide[:, c], wgv[:, c], start=(c == 0), stop=(c == DC - 1))
            last.then_inc(g_val_made, 1)
            pe.wait_ge(mm_split, 1)

            def queries(i, h, j):
                if j == 0:
                    pe.wait_ge(m_hi_done, i + 1)
                    pe.wait_ge(m_lo_done, i + 1)
                if inner(i - 1):
                    pe.wait_ge(q_taken, DC * (i - 1) + j + 1)
                at = slice(P * j, P * (j + 1))
                product(q_ps[:, j], lambda c: mm_hi[:, c, at], lambda c: mm_lo[:, c, at],
                        lambda c: m_hi[h][:, c], lambda c: m_lo[h][:, c]).then_inc(q_made, 1)

            def self_values(i, h, t):
                at = slice(P * t, P * (t + 1))
                if inner(i - 1) or t >= 2:
                    pe.wait_ge(e_done, LT * i + t - 1)
                product(e_ps[:, t % 2, 0:EW], lambda c: m_hi[h][:, c, at], lambda c: m_lo[h][:, c, at],
                        lambda c: wev_hi[:, c], lambda c: wev_lo[:, c]).then_inc(e_made, 1)

            def body(i, h):
                for j in range(DC):
                    queries(i, h, j)
                    if not inner(i - 1) and j == 0:
                        pe.wait_ge(wev_split, 2)
                    for t in range(2 * j, 2 * j + 2):
                        self_values(i, h, t)
            pieces(pe, body)
    return [(done, 16 * NL) for done in q_stored + e_stored]


def attention(nc, sb, pb, sem, x, mx, mask, out, q_dram, e_dram, k_hi, k_lo, v_hi, v_lo, g_val, one, consts,
              q_raw, q_in, mask_in, q_loaded, q_hi_done, q_split, mask_loaded, last_stores):
    ring = sb("ring", [P, GB, GW], FP32)
    p_hi = sb("p_hi", [P, 2, GW], F32R)
    p_lo = sb("p_lo", [P, 2, GW], F32R)
    top = sb("top", [P, GW], FP32)
    c_max = sb("c_max", [P, 2, QB], FP32)
    o_in = sb("o_in", [P, 2, QT, OW + 1], FP32)
    e_in = sb("e_in", [P, QT, EW], FP32)
    mx_in = sb("mx_in", [P, QT, D], FP32)
    y_rows = sb("y_rows", [P, QT, D], FP32)
    tops = sb("tops", [P, QT, 4], FP32)
    neg_max = sb("neg_max", [P, QT], FP32)
    part_w = sb("part_w", [P, QT, 4], FP32)
    part_sum = sb("part_sum", [P, QT, 4], FP32)
    prod = sb("prod", [P, QT, 4], FP32)
    denom = sb("denom", [P, QT], FP32)
    rden = sb("rden", [P, QT], FP32)
    share = sb("share", [P, QT, 4], FP32)
    stats = sb("stats", [P, QT, 6], FP32)
    mean_var = sb("mean_var", [P, QT, 2], FP32)
    var_eps = sb("var_eps", [P, QT], FP32)
    rstd = sb("rstd", [P, QT], FP32)
    shift = sb("shift", [P, QT], FP32)

    s_ps = pb("s_ps", [P, 2, GW])
    o_ps = pb("o_ps", [P, 2, QT, 512])

    mx_loaded, e_loaded, x_loaded, y_stored = sem("mx_loaded"), sem("e_loaded"), sem("x_loaded"), sem("y_stored")
    scores_ready, pv_done = sem("scores_ready"), sem("pv_done")
    slot_filled, chunk_max = sem("slot_filled"), sem("chunk_max")
    masked, top_steps, shifted, lo_ready = sem("masked"), sem("top_steps"), sem("shifted"), sem("lo_ready")
    exp_done, hi_ready = sem("exp_done"), sem("hi_ready")
    o_taken, part_w_ready, scaled, normed = sem("o_taken"), sem("part_w_ready"), sem("scaled"), sem("normed")
    negmax_steps, share_steps, merged, stat_steps, shift_ready = (
        sem("negmax_steps"), sem("share_steps"), sem("merged"), sem("stat_steps"), sem("shift_ready"))
    sums_ready, join_steps = sem("sums_ready"), sem("join_steps")
    summed, y_ready, rstd_steps = sem("summed"), sem("y_ready"), sem("rstd_steps")
    sp_passed, dve_passed, pool_passed = sem("sp_passed"), sem("dve_passed"), sem("pool_passed")
    TOPS = 5
    NEG, SHARE, STAT, SUMS, JOIN = 4, 4, 4, 3, 4 * QT

    def bodies(eng, body, first, last, end=NB):
        for b in range(first):
            body(b)
        with eng.Fori(first, end) as b:
            body(b)
        for b in range(end, last + 1):
            body(b)

    def group(b, j):
        g = b * GB + j
        return g if not isinstance(b, int) or 0 <= g < NG else None

    def ending(b, behind):
        return b - behind if not isinstance(b, int) or 0 <= b - behind < NB else None

    def closes(b):
        return isinstance(b, int) and b == NB - 1

    def drains(b):
        return isinstance(b, int) and b >= NB

    def short_end(e):
        return isinstance(e, int) and e == NB - 1

    def parts_joined(eng, e):
        if short_end(e):
            eng.wait_ge(join_steps, JOIN)
        elif started(e + 1):
            eng.wait_ge(summed, SUMS * (e + 1))

    rows = "(b t p) d -> b p t d"
    x_rows, mx_rows, out_rows = (a.rearrange(rows, t=QT, p=P) for a in (x, mx, out))

    block = nc.Block()
    with block:
        @block.sync
        def _(sp):
            for done, count in last_stores:
                sp.wait_ge(done, count)

            def body(b):
                here, one_back, two_back, three_back = (ending(b, n) for n in range(4))

                def mask_piece(m):
                    if started(GB * b + 2 * m - 2):
                        sp.wait_ge(masked, GB * b + 2 * m - 2)
                        held_apart(sp, b, sp_passed)
                    sp.dma_start(mask_in[:, m % 2], mask[b, m]).then_inc(mask_loaded[m % 2], 16)

                if here is not None and started(b):
                    mask_piece(0)
                if three_back is not None:
                    sp.wait_ge(normed, QT * (three_back + 1))
                    sp.dma_start(out_rows[three_back], y_rows[:]).then_inc(y_stored, 16)
                if here is not None:
                    if not (isinstance(b, int) and b + 1 >= NB):
                        sp.wait_ge(q_split, b + 1)
                        held_apart(sp, b, sp_passed)
                        sp.dma_start(q_raw[:], q_dram[bass.ds(b + 1, 1)].squeeze(0)).then_inc(q_loaded, 16)
                    if started(b):
                        mask_piece(1)
                if two_back is not None:
                    if started(two_back):
                        sp.wait_ge(merged, two_back)
                    sp.dma_start(mx_in[:], mx_rows[two_back]).then_inc(mx_loaded, 16)
                if here is not None:
                    mask_piece(2)
                if two_back is not None:
                    if short_end(two_back):
                        sp.wait_ge(y_stored, 16 * two_back)
                    else:
                        sp.wait_ge(summed, SUMS * (two_back + 1))
                    sp.dma_start(y_rows[:], x_rows[two_back]).then_inc(x_loaded, 16)
                if one_back is not None:
                    if started(one_back):
                        parts_joined(sp, one_back - 1)
                        held_apart(sp, b, sp_passed)
                        sp.wait_ge(e_loaded, 16 * one_back)
                    sp.dma_start(e_in[:], e_dram[one_back]).then_inc(e_loaded, 16)
                if here is not None:
                    mask_piece(3)
            bodies(sp, body, 3, NB + 2, NB - 1)
            sp.wait_ge(y_stored, 16 * NB)

        @block.tensor
        def _(pe):
            def scores(b, j):
                g = group(b, j)
                if g is None:
                    return
                if j == 0:
                    pe.wait_ge(q_split, b + 1)
                if started(g - 1):
                    pe.wait_ge(masked, g - 1)
                par = b % 2
                for k in range(GK):
                    tile = GK * j + k
                    at = slice(P * tile, P * (tile + 1))
                    steps = [(c, a, h) for c in range(DC) for a, h in ((k_hi, 0), (k_hi, 1), (k_lo, 0))]
                    for n, (c, a, h) in enumerate(steps):
                        q = q_in[:, par, h, c] if isinstance(b, int) else q_in[:, bass.ds(par, 1), h, c].squeeze(1)
                        last = nc.tensor.matmul(s_ps[:, j % 2, QB * k:QB * (k + 1)], a[:, c, at], q,
                                                start=(n == 0), stop=(n == len(steps) - 1))
                last.then_inc(scores_ready, 1)

            def weigh(b, j):
                p = group(b, j)
                if p is None:
                    return
                chunk = 2 * b + j // CG
                par = (j // CG) % 2
                pe.wait_ge(lo_ready, p + 1)
                if j % CG == 0:
                    if started(chunk - 1):
                        pe.wait_ge(o_taken, chunk - 1)
                    for t in range(QT):
                        nc.tensor.matmul(o_ps[:, par, t, D + 2:D + 3], c_max[0:1, par, P * t:P * (t + 1)],
                                         one[0:1, 0:1], start=True, stop=True)
                for k in range(GK):
                    tile = GK * (j % GB) + k
                    for t in range(QT):
                        o = o_ps[:, par, t]
                        at = slice(QB * k + P * t, QB * k + P * (t + 1))
                        first = j % CG == 0 and k == 0
                        final = j % CG == CG - 1 and k == GK - 1
                        nc.tensor.matmul(o[:, 0:VW], p_hi[:, j % 2, at], v_hi[:, tile], start=first, stop=False)
                        nc.tensor.matmul(o[:, 0:D], p_hi[:, j % 2, at], v_lo[:, tile], start=False, stop=False)
                        last = nc.tensor.matmul(o[:, 0:VW], p_lo[:, j % 2, at], v_hi[:, tile], start=False, stop=final)
                last.then_inc(pv_done, 1)

            def body(b):
                for j in range(GB):
                    scores(b, j)
                    weigh(b, j - LAG_PV)

            bodies(pe, body, 2, NB)

        @block.vector
        def _(dve):
            def shift_scores(b, j):
                p = group(b, j)
                if p is None:
                    return
                if j % CG == 0:
                    dve.wait_ge(chunk_max, 2 * b + j // CG + 1)
                s = ring[:, j % GB].rearrange("p (k q) -> p k q", q=QB)
                m = c_max[:, (j // CG) % 2].unsqueeze(1).broadcast_to([P, GK, QB])
                nc.vector.tensor_tensor(s, s, m, ALU.subtract).then_inc(shifted, 1)

            def mask_scores(b, j):
                g = group(b, j)
                if g is None:
                    return
                m = j // 2
                dve.wait_ge(scores_ready, g + 1)
                dve.wait_ge(slot_filled, g + 1)
                dve.wait_ge(mask_loaded[m % 2], 16 * (2 * b + m // 2 + 1))
                held_apart(dve, b, dve_passed)
                nc.vector.copy_predicated(ring[:, j], mask_in[:, m % 2, GW * (j % 2):GW * (j % 2 + 1)],
                                          s_ps[:, j % 2]).then_inc(masked, 1)

            def running_max(b, j):
                g, at, done = group(b, j), j % CG, TOPS * (2 * b + j // CG)
                if g is None or at == 0:
                    return
                dve.wait_ge(masked, g + 1)
                if at == 1:
                    if started(done):
                        dve.wait_ge(top_steps, done)
                        dve.wait_ge(chunk_max, 2 * b + j // CG)
                    nc.vector.tensor_tensor(top[:], ring[:, j - 1], ring[:, j], ALU.max).then_inc(top_steps, 1)
                else:
                    dve.wait_ge(top_steps, done + at - 1)
                    nc.vector.tensor_tensor(top[:], top[:], ring[:, j], ALU.max).then_inc(top_steps, 1)

            def fold_max(b, j):
                g, at, done = group(b, j), j % CG, TOPS * (2 * b + j // CG)
                if g is not None and at == CG - 1:
                    dve.wait_ge(top_steps, done + 3)
                    nc.vector.tensor_tensor(top[:, 0:2 * QB], top[:, 0:2 * QB], top[:, 2 * QB:4 * QB],
                                            ALU.max).then_inc(top_steps, 1)
                    dve.wait_ge(top_steps, done + 4)
                    nc.vector.tensor_tensor(top[:, 0:QB], top[:, 0:QB], top[:, QB:2 * QB], ALU.max).then_inc(top_steps, 1)

            def low_parts(b, j):
                p = group(b, j)
                if p is None:
                    return
                dve.wait_ge(hi_ready, p + 1)
                if started(p - 1):
                    dve.wait_ge(pv_done, p - 1)
                nc.vector.tensor_tensor(p_lo[:, j % 2], ring[:, j % GB], p_hi[:, j % 2], ALU.subtract).then_inc(lo_ready, 1)

            def row_max(e):
                dve.wait_ge(o_taken, 2 * (e + 1))
                dve.wait_ge(e_loaded, 16 * (e + 1))
                if started(e):
                    dve.wait_ge(part_w_ready, QT * e)
                for c in range(2):
                    nc.vector.tensor_copy(tops[:, :, c:c + 1], o_in[:, c, :, D + 2:D + 3]).then_inc(negmax_steps, 1)
                nc.vector.tensor_copy(tops[:, :, 2:4], e_in[:, :, D:D + 2]).then_inc(negmax_steps, 1)
                dve.wait_ge(negmax_steps, NEG * e + 3)
                nc.vector.tensor_reduce(neg_max[:], tops[:], AX, ALU.max, negate=True).then_inc(negmax_steps, 1)

            def shares(e):
                dve.wait_ge(part_w_ready, QT * (e + 1))
                dve.wait_ge(sums_ready, 2 * (e + 1))
                nc.vector.tensor_tensor(prod[:], part_w[:], part_sum[:], ALU.mult).then_inc(share_steps, 1)
                dve.wait_ge(share_steps, SHARE * e + 1)
                nc.vector.tensor_reduce(denom[:], prod[:], AX, ALU.add).then_inc(share_steps, 1)
                dve.wait_ge(share_steps, SHARE * e + 2)
                nc.vector.reciprocal(rden[:], denom[:]).then_inc(share_steps, 1)
                dve.wait_ge(share_steps, SHARE * e + 3)
                if started(e):
                    dve.wait_ge(scaled, 4 * QT * e)
                nc.vector.tensor_tensor(share[:], part_w[:], rden[:].unsqueeze(2).broadcast_to([P, QT, 4]),
                                        ALU.mult).then_inc(share_steps, 1)

            def join_parts(e):
                for n, part in enumerate((None, o_in[:, 0], e_in, g_val)):
                    for t in range(QT):
                        total = o_in[:, 1, t, 0:D]
                        if n == 0:
                            dve.wait_ge(share_steps, SHARE * (e + 1))
                            last = nc.vector.tensor_scalar(total, total, share[:, t, 1:2], None, ALU.mult)
                        else:
                            dve.wait_ge(join_steps, QT * (n - 1) + t + 1)
                            one_part = part[:] if n == 3 else part[:, t, 0:D]
                            last = nc.vector.scalar_tensor_tensor(total, one_part, share[:, t, (None, 0, 2, 3)[n]:(None, 1, 3, 4)[n]],
                                                                  total, ALU.mult, ALU.add)
                        last.then_inc(join_steps, 1)

            def merge(e):
                parts_joined(dve, e)
                dve.wait_ge(mx_loaded, 16 * (e + 1))
                nc.vector.tensor_tensor(o_in[:, 1, :, 0:D], o_in[:, 1, :, 0:D], mx_in[:], ALU.max).then_inc(merged, 1)
                if short_end(e):
                    dve.wait_ge(merged, e + 1)
                    dve.wait_ge(x_loaded, 16 * (e + 1))
                    nc.vector.tensor_tensor(o_in[:, 1, :, 0:D], o_in[:, 1, :, 0:D], y_rows[:], ALU.add).then_inc(y_ready, 1)

            def moments(e):
                dve.wait_ge(y_ready, e + 1)
                for t in range(QT):
                    nc.vector.bn_stats(stats[:, t], o_in[:, 1, t, 0:D]).then_inc(stat_steps, 1)
                dve.wait_ge(stat_steps, STAT * e + QT)
                if started(e):
                    dve.wait_ge(rstd_steps, 2 * e)
                    dve.wait_ge(shift_ready, e)
                    held_apart(dve, e, dve_passed)
                for t in range(QT):
                    nc.vector.bn_aggr(mean_var[:, t], stats[:, t]).then_inc(stat_steps, 1)

            def norm_shift(e):
                dve.wait_ge(stat_steps, STAT * (e + 1))
                dve.wait_ge(rstd_steps, 2 * (e + 1))
                if started(e):
                    dve.wait_ge(normed, QT * e)
                nc.vector.scalar_tensor_tensor(shift[:], mean_var[:, :, 0], -1.0, rstd[:], ALU.mult, ALU.mult).then_inc(shift_ready, 1)

            def body(b):
                one_back, two_back = ending(b, 1), ending(b, 2)
                closing, draining = closes(b), drains(b)
                for j in range(GB):
                    if j == 7 and closing:
                        row_max(one_back)
                    mask_scores(b, j)
                    if j == 0 and draining:
                        low_parts(b, j - LAG_LOW)
                    shift_scores(b, j - LAG_SHIFT)
                    if not (j == 0 and draining):
                        low_parts(b, j - LAG_LOW)
                    if j == 7 and closing:
                        shares(one_back)
                    running_max(b, j)
                    fold_max(b, j)
                    if two_back is not None:
                        early = 1 if draining and not short_end(two_back) else 0
                        if j == 0 - early:
                            shares(two_back)
                        if j == 3 - early:
                            if short_end(two_back):
                                join_parts(two_back)
                            merge(two_back)
                        if j == 4 - early:
                            moments(two_back)
                        if j == 5 - early:
                            norm_shift(two_back)
                    if j == 7 and one_back is not None and not closing:
                        row_max(one_back)

            bodies(dve, body, 3, NB + 1, NB - 1)

        @block.scalar
        def _(act):
            def queries_high(b):
                act.wait_ge(q_loaded, 16 * (b + 1))
                if started(GB * (b - 1)):
                    act.wait_ge(scores_ready, GB * (b - 1))
                nc.scalar.activation(q_in[:, bass.ds(b % 2, 1), 0].squeeze(1), q_raw[:], ACT.Copy).then_inc(q_hi_done, 1)

            def exponentials(b, j):
                p = group(b, j)
                if p is None:
                    return
                act.wait_ge(shifted, p + 1)
                nc.scalar.activation(ring[:, j % GB], ring[:, j % GB], ACT.Exp).then_inc(exp_done, 1)
                act.wait_ge(exp_done, p + 1)
                if started(p - 1):
                    act.wait_ge(pv_done, p - 1)
                nc.scalar.activation(p_hi[:, j % 2], ring[:, j % GB], ACT.Copy).then_inc(hi_ready, 1)

            def take_output(e, c):
                act.wait_ge(pv_done, CG * (2 * e + c + 1))
                if not started(e) and c == 0:
                    for done, count in last_stores:
                        act.wait_ge(done, count)
                if started(e) and c == 0:
                    parts_joined(act, e - 1)
                if started(e) and c == 1:
                    act.wait_ge(normed, QT * e)
                nc.scalar.activation(o_in[:, c, :, 0:OW], o_ps[:, c, :, 0:OW], ACT.Copy).then_inc(o_taken, 1)

            def part_weights(e):
                act.wait_ge(negmax_steps, NEG * e + 4)
                if started(e):
                    act.wait_ge(share_steps, SHARE * e)
                for t in range(QT):
                    nc.scalar.activation(part_w[:, t], tops[:, t], ACT.Exp, bias=neg_max[:, t:t + 1]).then_inc(part_w_ready, 1)

            def scale_parts(e):
                act.wait_ge(share_steps, SHARE * (e + 1))
                if started(e):
                    act.wait_ge(y_stored, 16 * e)
                for t in range(QT):
                    own = (o_in[:, 0, t, 0:D], o_in[:, 1, t, 0:D], e_in[:, t, 0:D])
                    for n, (part, to) in enumerate([(a, a) for a in own] + [(g_val[:], y_rows[:, t])]):
                        nc.scalar.activation(to, part, ACT.Copy, scale=share[:, t, n:n + 1]).then_inc(scaled, 1)

            def normalise(e):
                act.wait_ge(shift_ready, e + 1)
                for t in range(QT):
                    nc.scalar.activation(y_rows[:, t], o_in[:, 1, t, 0:D], ACT.Identity, bias=shift[:, t:t + 1],
                                         scale=rstd[:, t:t + 1]).then_inc(normed, 1)

            def body(b):
                one_back, two_back = ending(b, 1), ending(b, 2)
                for j in range(GB):
                    if two_back is not None:
                        early = drains(b) and not short_end(two_back)
                        if j == 0 and not early:
                            part_weights(two_back)
                        if j == 1 and not drains(b):
                            scale_parts(two_back)
                        if j == (5 if early else 6):
                            normalise(two_back)
                    if one_back is not None:
                        if j == 5:
                            take_output(one_back, 0)
                        if j == 7:
                            take_output(one_back, 1)
                    if j == 2 and ending(b, -1) is not None:
                        queries_high(b + 1)
                    if j == 7 and closes(b):
                        part_weights(one_back)
                    exponentials(b, j - LAG_SHIFT)
                    if j == 7 and closes(b):
                        scale_parts(one_back)

            bodies(act, body, 3, NB + 1, NB - 1)

        @block.gpsimd
        def _(pool):
            def fill(slot):
                nc.gpsimd.memset(ring[:, slot], MASKED).then_inc(slot_filled, 1)

            def queries_low(b):
                pool.wait_ge(q_hi_done, b + 1)
                if started(GB * (b - 1)):
                    pool.wait_ge(scores_ready, GB * (b - 1))
                q = q_in[:, bass.ds(b % 2, 1)].squeeze(1)
                nc.gpsimd.tensor_tensor(q[:, 1], q_raw[:], q[:, 0], ALU.subtract).then_inc(q_split, 1)

            def refill(b, j):
                p = group(b, j)
                if p is None or (isinstance(b, int) and p + GB >= NG):
                    return
                pool.wait_ge(lo_ready, p + 1)
                held_apart(pool, p, pool_passed)
                fill(j % GB)

            def all_max(b, j):
                g = group(b, j)
                if g is None:
                    return
                chunk, par = 2 * b + j // CG, j // CG
                pool.wait_ge(top_steps, TOPS * (chunk + 1))
                if started(chunk - 1):
                    pool.wait_ge(shifted, CG * (chunk - 1))
                    pool.wait_ge(pv_done, CG * (chunk - 2) + 1)
                    held_apart(pool, chunk, pool_passed)
                nc.gpsimd.partition_all_reduce(c_max[:, par], top[:, 0:QB], P, RMAX).then_inc(chunk_max, 1)

            def part_sums(e):
                pool.wait_ge(o_taken, 2 * (e + 1))
                if started(e):
                    pool.wait_ge(share_steps, SHARE * e)
                for c in range(2):
                    nc.gpsimd.tensor_tensor(part_sum[:, :, c:c + 1], o_in[:, c, :, D:D + 1], consts[:, 2:4].unsqueeze(2),
                                            ALU.mult).then_inc(sums_ready, 1)

            def sum_parts(e):
                pool.wait_ge(scaled, 4 * QT * (e + 1))
                nc.gpsimd.tensor_tensor(o_in[:, 1, :, 0:D], o_in[:, 1, :, 0:D], o_in[:, 0, :, 0:D], ALU.add).then_inc(summed, 1)
                pool.wait_ge(summed, SUMS * e + 1)
                nc.gpsimd.tensor_tensor(o_in[:, 1, :, 0:D], o_in[:, 1, :, 0:D], e_in[:, :, 0:D], ALU.add).then_inc(summed, 1)
                pool.wait_ge(summed, SUMS * e + 2)
                nc.gpsimd.tensor_tensor(o_in[:, 1, :, 0:D], o_in[:, 1, :, 0:D], y_rows[:], ALU.add).then_inc(summed, 1)

            def add_x(e):
                pool.wait_ge(merged, e + 1)
                pool.wait_ge(x_loaded, 16 * (e + 1))
                nc.gpsimd.tensor_tensor(o_in[:, 1, :, 0:D], o_in[:, 1, :, 0:D], y_rows[:], ALU.add).then_inc(y_ready, 1)

            def inverse_std(e):
                pool.wait_ge(stat_steps, STAT * (e + 1))
                if started(e):
                    pool.wait_ge(normed, QT * e)
                    held_apart(pool, e, pool_passed)
                nc.gpsimd.tensor_scalar(var_eps[:], mean_var[:, :, 1], EPS, 1.0, ALU.add, ALU.mult).then_inc(rstd_steps, 1)
                pool.wait_ge(rstd_steps, 2 * e + 1)
                nc.gpsimd.tensor_tensor(rstd[:], var_eps[:], consts[:, 0:2], ALU.pow).then_inc(rstd_steps, 1)

            for slot in range(GB):
                fill(slot)
            nc.gpsimd.memset(part_sum[:], 1.0).then_inc(pool_passed, 1)
            pool.wait_ge(pool_passed, 1)

            def body(b):
                one_back, two_back = ending(b, 1), ending(b, 2)
                for j in range(GB):
                    if two_back is not None:
                        if j == 2 and not short_end(two_back):
                            sum_parts(two_back)
                        if j == 4 and not short_end(two_back):
                            add_x(two_back)
                        if j == 5:
                            inverse_std(two_back)
                    refill(b, j - LAG_LOW)
                    if j == 7 and one_back is not None:
                        part_sums(one_back)
                    if j % CG == CG - 1:
                        all_max(b, j)
                    if j == 3 and ending(b, -1) is not None:
                        queries_low(b + 1)

            bodies(pool, body, 3, NB + 1, NB - 1)


def kernel(**inputs):
    import numpy as np
    import concourse.bacc as bacc
    from concourse.bass_utils import run_bass_kernel_spmd

    nc = bacc.Bacc("TRN2", target_bir_lowering=False, num_devices=1)
    arrays = {}

    def given(name, a):
        a = np.ascontiguousarray(a)
        arrays["in_" + name] = a
        return nc.dram_tensor("in_" + name, a.shape, mybir.dt.from_np(a.dtype), kind="ExternalInput").ap()

    x = np.asarray(inputs["x"])
    mx = np.asarray(inputs["L0_gnn_masked_x"])
    adj = np.asarray(inputs["adj"])
    mask = adj.T.reshape(GB // 2, 2 * GK, P, NB, QB).transpose(3, 0, 2, 1, 4).reshape(NB, GB // 2, P, 2 * GW)
    w = {}
    for name in ("Wlv", "blv", "Wgk", "Wgv", "bgv", "Wes", "Wev", "bev"):
        w[name] = given(name, np.asarray(inputs["L0_gnn_" + name]))
    for name in ("Wlq", "Wlk", "Wgq"):
        w[name + "T"] = given(name + "T", np.asarray(inputs["L0_gnn_" + name]).T)
    args = [given("x", x), given("xT", x.T), given("mxT", mx.T), given("mx", mx), given("mask", mask)]
    out = nc.dram_tensor("result", (N, D), FP32, kind="ExternalOutput").ap()
    build(nc, *args, w, out)
    r = run_bass_kernel_spmd(nc, [arrays], core_ids=[0])
    return r.results[0]["result"]
```
